# Optimizing a Trainium2 kernel written in Bass

```python
import numpy as np
import jax
import jax.numpy as jnp

def _softmax(x, axis=-1):
    return jax.nn.softmax(x, axis=axis)

def _gelu(x):
    return jax.nn.gelu(x, approximate=True)

def _silu(x):
    return jax.nn.silu(x)

def _sigmoid(x):
    return jax.nn.sigmoid(x)

def _layernorm(x, axis=-1, eps=1e-05):
    m = jnp.mean(x, axis=axis, keepdims=True)
    v = jnp.var(x, axis=axis, keepdims=True)
    return (x - m) / jnp.sqrt(v + eps)

def _scatter_add(tgt, idx, src, axis=0):
    return tgt.at[idx].add(src)

def _segment_sum(src, seg, n):
    return jax.ops.segment_sum(src, seg, n)
kernel_name = 'mk_xattn_ffn_d4_seqx_r8_99d41a'

def setup_inputs(seed: int=0):
    np.random.seed(seed)
    _w = jnp.asarray

    def _rec_inputs():
        import jax
        import jax.numpy as jnp
        _rk = jax.random.key(seed)
        x = 7.22e-05 + 1 * jax.random.normal(jax.random.fold_in(_rk, 1), (64, 64, 128), jnp.float32)
        _lenS = 64 - jax.random.randint(jax.random.fold_in(_rk, 7), (64,), 0, max(1, 64 // 4) + 1, jnp.int32)
        _lenS2 = 64 - jax.random.randint(jax.random.fold_in(_rk, 8), (64,), 0, max(1, 64 // 4) + 1, jnp.int32)
        _ctx_1024P = jax.random.normal(jax.random.fold_in(_rk, 11), (64, 16, 128), jnp.float32)
        _ctx_1024c = jax.random.dirichlet(jax.random.fold_in(_rk, 511), 0.3 * jnp.ones((16,), jnp.float32), (64, 64))
        _ctx_1024t = jnp.einsum('bsk,bkd->bsd', _ctx_1024c, _ctx_1024P)
        _ctx_1024t = _ctx_1024t * jax.lax.rsqrt(jnp.mean(jnp.square(_ctx_1024t)) + 1e-12) * 0.953939
        ctx_1024 = 4.13588e-05 + 0.999923 * (_ctx_1024t + 0.3 * jax.random.normal(jax.random.fold_in(_rk, 611), (64, 64, 128), jnp.float32))
        _validS = jnp.arange(64)[None, :] < _lenS[:, None]
        _validS2 = jnp.arange(64)[None, :] < _lenS2[:, None]
        _causal = jnp.tril(jnp.ones((64, 64), dtype=bool))
        mask_BxS2_bk0 = jnp.logical_not(jnp.broadcast_to(_validS2[:, :], (64, 64)))
        return (x, ctx_1024, mask_BxS2_bk0)
    x, ctx_1024, mask_BxS2_bk0 = _rec_inputs()

    def _L0_xattn_setup():
        import jax, jax.numpy as jnp
        import numpy as np
        D_MODEL = 128
        HEADS = 16
        D_HEAD = D_MODEL // HEADS
        SEQ = 256
        C = 2
        K_TOP = int(C * np.log(SEQ))
        key = jax.random.key(seed)
        ks = jax.random.split(key, 5)
        s = 0.02
        return {'Q': jax.random.normal(ks[0], (4, SEQ, D_MODEL), jnp.float32), 'K': jax.random.normal(ks[1], (4, SEQ, D_MODEL), jnp.float32), 'V': jax.random.normal(ks[2], (4, SEQ, D_MODEL), jnp.float32), 'Wq': jax.random.normal(ks[3], (D_MODEL, D_HEAD), jnp.float32) * s, 'bq': jnp.zeros((D_HEAD,), jnp.float32), 'Wout': jax.random.normal(ks[4], (HEADS * D_HEAD, D_MODEL), jnp.float32) * s, 'bout': jnp.zeros((D_MODEL,), jnp.float32)}
    _L0_xattn_all = _L0_xattn_setup()
    _L0_xattn_in = {k: v for k, v in _L0_xattn_all.items() if k in ('Wq', 'bq', 'Wout', 'bout')}
    del _L0_xattn_all

    def _L0_ffn_setup():
        import jax, jax.numpy as jnp
        import numpy as np
        D_MODEL = 128
        HIDDEN = 512
        N_EXPERTS = 8
        TOP_K = 2
        key = jax.random.key(seed)
        k_x, k_r, k_w1, k_w2 = jax.random.split(key, 4)
        x = jax.random.normal(k_x, (2, 128, D_MODEL), dtype=jnp.float32)
        Wr = jax.random.normal(k_r, (D_MODEL, N_EXPERTS), dtype=jnp.float32) * 0.02
        W1 = jax.random.normal(k_w1, (N_EXPERTS, D_MODEL, HIDDEN), dtype=jnp.float32) * 0.02
        W2 = jax.random.normal(k_w2, (N_EXPERTS, HIDDEN, D_MODEL), dtype=jnp.float32) * 0.02
        return {'x': x, 'Wr': Wr, 'W1': W1, 'W2': W2}
    _L0_ffn_all = _L0_ffn_setup()
    _L0_ffn_in = {k: v for k, v in _L0_ffn_all.items() if k in ('Wr', 'W1', 'W2')}
    del _L0_ffn_all

    def _L1_xattn_setup():
        import jax, jax.numpy as jnp
        import numpy as np
        B, S, DIM, NH = (2, 256, 128, 8)
        DH = DIM // NH
        GATE_SOFT_CAP = 15.0
        BACKEND_EPS = 5e-05
        NORM_EPS = 1e-06

        def _mlstm_parallel(q, k, v, i_pre, f_pre):
            log_fg = jax.nn.log_sigmoid(f_pre)
            lf_cs = jnp.cumsum(log_fg, axis=-1)
            lf = jnp.concatenate([jnp.zeros_like(lf_cs[..., :1]), lf_cs], axis=-1)
            log_d = lf[..., 1:, None] - lf[..., None, 1:] + i_pre[..., None, :]
            t_idx = jnp.arange(q.shape[2])
            mask = t_idx[:, None] >= t_idx[None, :]
            log_d = jnp.where(mask, log_d, -jnp.inf)
            m = jnp.max(log_d, axis=-1, keepdims=True)
            d_mat = jnp.exp(log_d - m)
            scores = jnp.einsum('bhtd,bhsd->bhts', q, k) * (1.0 / np.sqrt(DH))
            s_mat = scores * d_mat
            denom = jnp.maximum(jnp.abs(jnp.sum(s_mat, axis=-1, keepdims=True)), jnp.exp(-m)) + BACKEND_EPS
            return jnp.einsum('bhts,bhsd->bhtd', s_mat, v) / denom
        key = jax.random.key(seed)
        kq, kk, kv, kw = jax.random.split(key, 4)
        q = jax.random.normal(kq, (B, S, DIM), dtype=jnp.float32)
        k = jax.random.normal(kk, (B, S, DIM), dtype=jnp.float32)
        v = jax.random.normal(kv, (B, S, DIM), dtype=jnp.float32)
        ifgate_w = 0.02 * jax.random.normal(kw, (2 * NH, 3 * DIM), dtype=jnp.float32)
        ifgate_b = jnp.concatenate([jnp.full((NH,), -10.0, dtype=jnp.float32), jnp.linspace(3.0, 6.0, NH, dtype=jnp.float32)])
        outnorm_w = jnp.zeros((DIM,), dtype=jnp.float32)
        return {'q': q, 'k': k, 'v': v, 'ifgate_w': ifgate_w, 'ifgate_b': ifgate_b, 'outnorm_w': outnorm_w}
    _L1_xattn_all = _L1_xattn_setup()
    _L1_xattn_in = {k: v for k, v in _L1_xattn_all.items() if k in ('ifgate_w', 'ifgate_b', 'outnorm_w')}
    del _L1_xattn_all

    def _L1_ffn_setup():
        import jax, jax.numpy as jnp
        import numpy as np
        NUM_EXPERTS = 8
        NUM_LANGS = 4
        TOP_K = 2
        D_MODEL = 128
        EXPERT_SIZE = 512
        B, S = (2, 256)
        key = jax.random.key(seed)
        ks = jax.random.split(key, 6)

        def xavier(k, shape, fan_in, fan_out):
            a = float(np.sqrt(6.0 / (fan_in + fan_out)))
            return jax.random.uniform(k, shape, jnp.float32, -a, a)
        return {'x': jax.random.normal(ks[0], (B, S, D_MODEL), jnp.float32), 'router_w': xavier(ks[1], (NUM_EXPERTS, D_MODEL), D_MODEL, NUM_EXPERTS), 'router_b': jnp.zeros((NUM_EXPERTS,), jnp.float32), 'lang_w': xavier(ks[2], (NUM_LANGS, D_MODEL), D_MODEL, NUM_LANGS), 'lang_b': jnp.zeros((NUM_LANGS,), jnp.float32), 'w1': xavier(ks[3], (NUM_EXPERTS, D_MODEL, EXPERT_SIZE), D_MODEL, EXPERT_SIZE), 'b1': jnp.zeros((NUM_EXPERTS, EXPERT_SIZE), jnp.float32), 'w2': xavier(ks[4], (NUM_EXPERTS, EXPERT_SIZE, D_MODEL), EXPERT_SIZE, D_MODEL), 'b2': jnp.zeros((NUM_EXPERTS, D_MODEL), jnp.float32)}
    _L1_ffn_all = _L1_ffn_setup()
    _L1_ffn_in = {k: v for k, v in _L1_ffn_all.items() if k in ('router_w', 'router_b', 'lang_w', 'lang_b', 'w1', 'b1', 'w2', 'b2')}
    del _L1_ffn_all

    def _L2_xattn_setup():
        import jax, jax.numpy as jnp
        import numpy as np
        B, LQ, LKV = (8, 128, 256)
        QDIM, KDIM, HID = (128, 128, 128)
        key = jax.random.key(seed)
        ks = jax.random.split(key, 12)
        s = lambda d: 1.0 / np.sqrt(d)
        return {'query': jax.random.normal(ks[0], (B, LQ, QDIM), jnp.float32), 'key_value': jax.random.normal(ks[1], (B, LKV, KDIM), jnp.float32), 'key_mask': jax.random.randint(ks[2], (B, LKV), 0, 2).astype(bool), 'Wq': jax.random.uniform(ks[3], (QDIM, HID), jnp.float32, -s(QDIM), s(QDIM)), 'bq': jax.random.uniform(ks[4], (HID,), jnp.float32, -s(QDIM), s(QDIM)), 'Wk': jax.random.uniform(ks[5], (KDIM, HID), jnp.float32, -s(KDIM), s(KDIM)), 'bk': jax.random.uniform(ks[6], (HID,), jnp.float32, -s(KDIM), s(KDIM)), 'Wv': jax.random.uniform(ks[7], (KDIM, HID), jnp.float32, -s(KDIM), s(KDIM)), 'bv': jax.random.uniform(ks[8], (HID,), jnp.float32, -s(KDIM), s(KDIM)), 'Wo': jax.random.uniform(ks[9], (HID, QDIM), jnp.float32, -s(HID), s(HID)), 'bo': jax.random.uniform(ks[10], (QDIM,), jnp.float32, -s(HID), s(HID))}
    _L2_xattn_all = _L2_xattn_setup()
    _L2_xattn_in = {k: v for k, v in _L2_xattn_all.items() if k in ('Wq', 'bq', 'Wk', 'bk', 'Wv', 'bv', 'Wo', 'bo')}
    del _L2_xattn_all

    def _L2_ffn_setup():
        import jax, jax.numpy as jnp
        import numpy as np
        E = 16
        F_C = 2.0
        D = 128
        I = 4 * D
        IS = 2 * D
        B, S = (4, 128)
        key = jax.random.key(seed)
        ks = jax.random.split(key, 8)
        w = 0.02
        return {'hidden_states': jax.random.normal(ks[0], (B, S, D), dtype=jnp.float32), 'gate_w': jax.random.normal(ks[1], (E, D), dtype=jnp.float32) * w, 'Wg': jax.random.normal(ks[2], (E, I, D), dtype=jnp.float32) * w, 'Wu': jax.random.normal(ks[3], (E, I, D), dtype=jnp.float32) * w, 'Wd': jax.random.normal(ks[4], (E, D, I), dtype=jnp.float32) * w, 'Sg': jax.random.normal(ks[5], (IS, D), dtype=jnp.float32) * w, 'Su': jax.random.normal(ks[6], (IS, D), dtype=jnp.float32) * w, 'Sd': jax.random.normal(ks[7], (D, IS), dtype=jnp.float32) * w}
    _L2_ffn_all = _L2_ffn_setup()
    _L2_ffn_in = {k: v for k, v in _L2_ffn_all.items() if k in ('gate_w', 'Wg', 'Wu', 'Wd', 'Sg', 'Su', 'Sd')}
    del _L2_ffn_all

    def _L3_xattn_setup():
        import jax, jax.numpy as jnp
        import numpy as np
        DIM = 128
        HEADS = 16
        HEAD_DIM = DIM // HEADS
        B, N, S = (4, 512, 64)
        key = jax.random.key(seed)
        ks = jax.random.split(key, 9)
        scale = DIM ** (-0.5)
        return {'x': jax.random.normal(ks[0], (B, N, DIM), dtype=jnp.float32), 'context': jax.random.normal(ks[1], (B, S, DIM), dtype=jnp.float32), 'context_mask': jax.random.uniform(ks[2], (B, S)) < 0.2, 'q_w': jax.random.normal(ks[3], (DIM, DIM), dtype=jnp.float32) * scale, 'q_b': jnp.zeros((DIM,), dtype=jnp.float32), 'kv_w': jax.random.normal(ks[4], (DIM, 2 * DIM), dtype=jnp.float32) * scale, 'kv_b': jnp.zeros((2 * DIM,), dtype=jnp.float32), 'proj_w': jax.random.normal(ks[5], (DIM, DIM), dtype=jnp.float32) * scale, 'proj_b': jnp.zeros((DIM,), dtype=jnp.float32)}
    _L3_xattn_all = _L3_xattn_setup()
    _L3_xattn_in = {k: v for k, v in _L3_xattn_all.items() if k in ('q_w', 'q_b', 'kv_w', 'kv_b', 'proj_w', 'proj_b')}
    del _L3_xattn_all

    def _L3_ffn_setup():
        import jax, jax.numpy as jnp
        import numpy as np
        EMBED = 128
        D_FF = 4 * EMBED
        N_EXPERTS = 8
        TOP_K = 2
        B, S = (2, 128)
        key = jax.random.key(seed)
        ks = jax.random.split(key, 10)
        sc_d = 1.0 / np.sqrt(EMBED)
        sc_h = 1.0 / np.sqrt(D_FF)
        return {'inputs': jax.random.normal(ks[0], (B, S, EMBED), jnp.float32), 'rw1': jax.random.normal(ks[1], (EMBED, D_FF), jnp.float32) * sc_d, 'rb1': jnp.zeros((D_FF,), jnp.float32), 'rw2': jax.random.normal(ks[2], (D_FF, N_EXPERTS), jnp.float32) * sc_h, 'rb2': jnp.zeros((N_EXPERTS,), jnp.float32), 'W1': jax.random.normal(ks[3], (N_EXPERTS, EMBED, D_FF), jnp.float32) * sc_d, 'b1': jnp.zeros((N_EXPERTS, D_FF), jnp.float32), 'W2': jax.random.normal(ks[4], (N_EXPERTS, D_FF, EMBED), jnp.float32) * sc_h, 'b2': jnp.zeros((N_EXPERTS, EMBED), jnp.float32)}
    _L3_ffn_all = _L3_ffn_setup()
    _L3_ffn_in = {k: v for k, v in _L3_ffn_all.items() if k in ('rw1', 'rb1', 'rw2', 'rb2', 'W1', 'b1', 'W2', 'b2')}
    del _L3_ffn_all
    return {'x': x, 'ctx_1024': ctx_1024, 'mask_BxS2_bk0': mask_BxS2_bk0, 'L0_xattn_Wq': _L0_xattn_in['Wq'], 'L0_xattn_bq': _L0_xattn_in['bq'], 'L0_xattn_Wout': _L0_xattn_in['Wout'], 'L0_xattn_bout': _L0_xattn_in['bout'], 'L0_ffn_Wr': _L0_ffn_in['Wr'], 'L0_ffn_W1': _L0_ffn_in['W1'], 'L0_ffn_W2': _L0_ffn_in['W2'], 'L1_xattn_ifgate_w': _L1_xattn_in['ifgate_w'], 'L1_xattn_ifgate_b': _L1_xattn_in['ifgate_b'], 'L1_xattn_outnorm_w': _L1_xattn_in['outnorm_w'], 'L1_ffn_router_w': _L1_ffn_in['router_w'], 'L1_ffn_router_b': _L1_ffn_in['router_b'], 'L1_ffn_lang_w': _L1_ffn_in['lang_w'], 'L1_ffn_lang_b': _L1_ffn_in['lang_b'], 'L1_ffn_w1': _L1_ffn_in['w1'], 'L1_ffn_b1': _L1_ffn_in['b1'], 'L1_ffn_w2': _L1_ffn_in['w2'], 'L1_ffn_b2': _L1_ffn_in['b2'], 'L2_xattn_Wq': _L2_xattn_in['Wq'], 'L2_xattn_bq': _L2_xattn_in['bq'], 'L2_xattn_Wk': _L2_xattn_in['Wk'], 'L2_xattn_bk': _L2_xattn_in['bk'], 'L2_xattn_Wv': _L2_xattn_in['Wv'], 'L2_xattn_bv': _L2_xattn_in['bv'], 'L2_xattn_Wo': _L2_xattn_in['Wo'], 'L2_xattn_bo': _L2_xattn_in['bo'], 'L2_ffn_gate_w': _L2_ffn_in['gate_w'], 'L2_ffn_Wg': _L2_ffn_in['Wg'], 'L2_ffn_Wu': _L2_ffn_in['Wu'], 'L2_ffn_Wd': _L2_ffn_in['Wd'], 'L2_ffn_Sg': _L2_ffn_in['Sg'], 'L2_ffn_Su': _L2_ffn_in['Su'], 'L2_ffn_Sd': _L2_ffn_in['Sd'], 'L3_xattn_q_w': _L3_xattn_in['q_w'], 'L3_xattn_q_b': _L3_xattn_in['q_b'], 'L3_xattn_kv_w': _L3_xattn_in['kv_w'], 'L3_xattn_kv_b': _L3_xattn_in['kv_b'], 'L3_xattn_proj_w': _L3_xattn_in['proj_w'], 'L3_xattn_proj_b': _L3_xattn_in['proj_b'], 'L3_ffn_rw1': _L3_ffn_in['rw1'], 'L3_ffn_rb1': _L3_ffn_in['rb1'], 'L3_ffn_rw2': _L3_ffn_in['rw2'], 'L3_ffn_rb2': _L3_ffn_in['rb2'], 'L3_ffn_W1': _L3_ffn_in['W1'], 'L3_ffn_b1': _L3_ffn_in['b1'], 'L3_ffn_W2': _L3_ffn_in['W2'], 'L3_ffn_b2': _L3_ffn_in['b2']}

def reference(x, ctx_1024, mask_BxS2_bk0, L0_xattn_Wq, L0_xattn_bq, L0_xattn_Wout, L0_xattn_bout, L0_ffn_Wr, L0_ffn_W1, L0_ffn_W2, L1_xattn_ifgate_w, L1_xattn_ifgate_b, L1_xattn_outnorm_w, L1_ffn_router_w, L1_ffn_router_b, L1_ffn_lang_w, L1_ffn_lang_b, L1_ffn_w1, L1_ffn_b1, L1_ffn_w2, L1_ffn_b2, L2_xattn_Wq, L2_xattn_bq, L2_xattn_Wk, L2_xattn_bk, L2_xattn_Wv, L2_xattn_bv, L2_xattn_Wo, L2_xattn_bo, L2_ffn_gate_w, L2_ffn_Wg, L2_ffn_Wu, L2_ffn_Wd, L2_ffn_Sg, L2_ffn_Su, L2_ffn_Sd, L3_xattn_q_w, L3_xattn_q_b, L3_xattn_kv_w, L3_xattn_kv_b, L3_xattn_proj_w, L3_xattn_proj_b, L3_ffn_rw1, L3_ffn_rb1, L3_ffn_rw2, L3_ffn_rb2, L3_ffn_W1, L3_ffn_b1, L3_ffn_W2, L3_ffn_b2):
    import jax
    import jax.numpy as jnp

    def _L0_xattn_ref(Q, K, V, Wq, bq, Wout, bout):
        import jax, jax.numpy as jnp
        import numpy as np
        D_MODEL = 128
        HEADS = 16
        D_HEAD = D_MODEL // HEADS
        SEQ = 256
        C = 2
        K_TOP = int(C * np.log(SEQ))
        B, L, _ = Q.shape
        q = (Q @ Wq + bq).transpose(0, 2, 1)
        k_ = (K @ Wq + bq).transpose(0, 2, 1)
        v = (V @ Wq + bq).transpose(0, 2, 1)
        Qf = jnp.fft.fft(q.astype(jnp.complex64))
        Kf = jnp.fft.fft(k_.astype(jnp.complex64))
        corr = jnp.real(jnp.fft.ifft(Qf * jnp.conj(Kf)))
        corr = corr.mean(axis=(0, 1))
        W_topk, I_topk = jax.lax.top_k(corr, K_TOP)
        W_topk = jax.nn.softmax(W_topk)

        def body(R, ws):
            w, shift = ws
            return (R + w * jnp.roll(v, -shift, axis=-1), None)
        R3, _ = jax.lax.scan(body, jnp.zeros_like(v), (W_topk, I_topk))
        R = jnp.broadcast_to(R3[:, None], (B, HEADS, D_HEAD, L)).reshape(B, L, HEADS * D_HEAD)
        return R @ Wout + bout

    def _L0_ffn_ref(x, Wr, W1, W2):
        import jax, jax.numpy as jnp
        import numpy as np
        D_MODEL = 128
        HIDDEN = 512
        N_EXPERTS = 8
        TOP_K = 2
        B, S, D = x.shape
        flat = x.reshape(-1, D)
        logits = flat @ Wr
        top_vals, top_idx = jax.lax.top_k(logits, TOP_K)
        weights = jax.nn.softmax(top_vals, axis=-1)
        top1 = top_idx[:, 0]
        w_top1 = weights[:, 0]
        h = jax.nn.gelu(jnp.einsum('td,edh->teh', flat, W1), approximate=False)
        y = jnp.einsum('teh,ehd->ted', h, W2)
        y_sel = jnp.take_along_axis(y, top1[:, None, None], axis=1)[:, 0, :]
        out = (w_top1[:, None] * y_sel).reshape(B, S, D)
        return out

    def _L1_xattn_ref(q, k, v, ifgate_w, ifgate_b, outnorm_w):
        import jax, jax.numpy as jnp
        import numpy as np
        B, S, DIM, NH = (2, 256, 128, 8)
        DH = DIM // NH
        GATE_SOFT_CAP = 15.0
        BACKEND_EPS = 5e-05
        NORM_EPS = 1e-06

        def _mlstm_parallel(q, k, v, i_pre, f_pre):
            log_fg = jax.nn.log_sigmoid(f_pre)
            lf_cs = jnp.cumsum(log_fg, axis=-1)
            lf = jnp.concatenate([jnp.zeros_like(lf_cs[..., :1]), lf_cs], axis=-1)
            log_d = lf[..., 1:, None] - lf[..., None, 1:] + i_pre[..., None, :]
            t_idx = jnp.arange(q.shape[2])
            mask = t_idx[:, None] >= t_idx[None, :]
            log_d = jnp.where(mask, log_d, -jnp.inf)
            m = jnp.max(log_d, axis=-1, keepdims=True)
            d_mat = jnp.exp(log_d - m)
            scores = jnp.einsum('bhtd,bhsd->bhts', q, k) * (1.0 / np.sqrt(DH))
            s_mat = scores * d_mat
            denom = jnp.maximum(jnp.abs(jnp.sum(s_mat, axis=-1, keepdims=True)), jnp.exp(-m)) + BACKEND_EPS
            return jnp.einsum('bhts,bhsd->bhtd', s_mat, v) / denom
        b, s, dim = q.shape
        gate_in = jnp.concatenate([q, k, v], axis=-1)
        pre = gate_in @ ifgate_w.T + ifgate_b
        pre = GATE_SOFT_CAP * jnp.tanh(pre / GATE_SOFT_CAP)
        i_pre = pre[..., :NH].transpose(0, 2, 1)
        f_pre = pre[..., NH:].transpose(0, 2, 1)
        qh = q.reshape(b, s, NH, DH).transpose(0, 2, 1, 3)
        kh = k.reshape(b, s, NH, DH).transpose(0, 2, 1, 3)
        vh = v.reshape(b, s, NH, DH).transpose(0, 2, 1, 3)
        h = _mlstm_parallel(qh, kh, vh, i_pre, f_pre)
        rrms = jax.lax.rsqrt(jnp.mean(h * h, axis=-1, keepdims=True) + NORM_EPS)
        gain = (1.0 + outnorm_w).reshape(1, NH, 1, DH)
        h = h * rrms * gain
        return h.transpose(0, 2, 1, 3).reshape(b, s, dim)

    def _L1_ffn_ref(x, router_w, router_b, lang_w, lang_b, w1, b1, w2, b2):
        import jax, jax.numpy as jnp
        import numpy as np
        NUM_EXPERTS = 8
        NUM_LANGS = 4
        TOP_K = 2
        D_MODEL = 128
        EXPERT_SIZE = 512
        B, S = (2, 256)
        lang_logits = x @ lang_w.T + lang_b
        lang_probs = jax.nn.softmax(lang_logits, axis=-1)
        lp_pad = jnp.pad(lang_probs, ((0, 0), (0, 0), (0, 1)))
        idx = jnp.arange(NUM_EXPERTS) % NUM_LANGS
        expert_weights = lp_pad[..., idx] + lp_pad[..., idx + 1]
        router_logits = x @ router_w.T + router_b + 0.1 * expert_weights
        router_probs = jax.nn.softmax(router_logits, axis=-1)
        top_p, top_i = jax.lax.top_k(router_probs, TOP_K)
        top_p = top_p / top_p.sum(axis=-1, keepdims=True)
        h = jax.nn.gelu(jnp.einsum('bsd,edh->bseh', x, w1) + b1, approximate=False)
        expert_out = jnp.einsum('bseh,ehd->bsed', h, w2) + b2
        sel = jnp.take_along_axis(expert_out, top_i[..., None], axis=2)
        return (top_p[..., None] * sel).sum(axis=2)

    def _L2_xattn_ref(query, key_value, key_mask, Wq, bq, Wk, bk, Wv, bv, Wo, bo):
        import jax, jax.numpy as jnp
        import numpy as np
        B, LQ, LKV = (8, 128, 256)
        QDIM, KDIM, HID = (128, 128, 128)
        Q = query @ Wq + bq
        K = key_value @ Wk + bk
        V = key_value @ Wv + bv
        hid = Q.shape[-1]
        scores = jnp.einsum('bqh,bkh->bqk', Q, K) / jnp.sqrt(jnp.float32(hid))
        scores = jnp.where(key_mask[:, None, :], scores, jnp.float32(-1000000000.0))
        attn = jax.nn.softmax(scores, axis=-1)
        context = jnp.einsum('bqk,bkh->bqh', attn, V)
        return context @ Wo + bo

    def _L2_ffn_ref(hidden_states, gate_w, Wg, Wu, Wd, Sg, Su, Sd):
        import jax, jax.numpy as jnp
        import numpy as np
        E = 16
        F_C = 2.0
        D = 128
        I = 4 * D
        IS = 2 * D
        B, S = (4, 128)
        b, s, d = hidden_states.shape
        T = b * s
        C = int(T * F_C / E)
        flat_x = hidden_states.reshape(T, d)
        logits = flat_x @ gate_w.T
        scores = jax.nn.softmax(logits, axis=-1).T
        topk_weight, topk_idx = jax.lax.top_k(scores, C)
        xg = flat_x[topk_idx]
        g = jnp.einsum('ecd,eid->eci', xg, Wg)
        u = jnp.einsum('ecd,eid->eci', xg, Wu)
        h = jax.nn.gelu(g, approximate=False) * u
        eo = jnp.einsum('eci,edi->ecd', h, Wd)
        eo = eo * topk_weight[..., None]
        flat_out = jnp.zeros_like(flat_x).at[topk_idx.reshape(-1)].add(eo.reshape(-1, d))
        out = flat_out.reshape(b, s, d)
        sg = hidden_states @ Sg.T
        su = hidden_states @ Su.T
        shared = jax.nn.gelu(sg, approximate=False) * su @ Sd.T
        return out + shared

    def _L3_xattn_ref(x, context, context_mask, q_w, q_b, kv_w, kv_b, proj_w, proj_b):
        import jax, jax.numpy as jnp
        import numpy as np
        DIM = 128
        HEADS = 16
        HEAD_DIM = DIM // HEADS
        B, N, S = (4, 512, 64)
        b, n, c = x.shape
        s = context.shape[1]
        h, d = (HEADS, HEAD_DIM)
        scale = d ** (-0.5)
        q = (x @ q_w + q_b).reshape(b, n, h, d)
        kv = (context @ kv_w + kv_b).reshape(b, s, 2, h, d)
        k = kv[:, :, 0]
        v = kv[:, :, 1]
        attn = jnp.einsum('bnhd,bshd->bhns', q, k) * scale
        attn = jnp.where(context_mask[:, None, None, :], -jnp.inf, attn)
        attn = jax.nn.softmax(attn, axis=-1)
        out = jnp.einsum('bhns,bshd->bnhd', attn, v).reshape(b, n, c)
        return out @ proj_w + proj_b

    def _L3_ffn_ref(inputs, rw1, rb1, rw2, rb2, W1, b1, W2, b2):
        import jax, jax.numpy as jnp
        import numpy as np
        EMBED = 128
        D_FF = 4 * EMBED
        N_EXPERTS = 8
        TOP_K = 2
        B, S = (2, 128)
        Bb, Ss, D = inputs.shape
        T = Bb * Ss
        xf = inputs.reshape(T, D)
        score = jax.nn.relu(xf @ rw1 + rb1) @ rw2 + rb2
        _, topi = jax.lax.top_k(score, TOP_K)
        mask = jnp.zeros(score.shape, bool).at[jnp.arange(T)[:, None], topi].set(True)
        gate = jax.nn.softmax(jnp.where(mask, score, -jnp.inf), axis=-1)
        out = jnp.zeros_like(xf)
        for e in range(N_EXPERTS):
            h = jax.nn.relu(xf @ W1[e] + b1[e])
            y = h @ W2[e] + b2[e]
            out = out + gate[:, e:e + 1] * y
        return out.reshape(Bb, Ss, D)
    x = x + _L0_xattn_ref(_layernorm(x, axis=-1), ctx_1024, ctx_1024, L0_xattn_Wq, L0_xattn_bq, L0_xattn_Wout, L0_xattn_bout)
    x = x + _L0_ffn_ref(_layernorm(x, axis=-1), L0_ffn_Wr, L0_ffn_W1, L0_ffn_W2)
    x = x + _L1_xattn_ref(_layernorm(x, axis=-1), ctx_1024, ctx_1024, L1_xattn_ifgate_w, L1_xattn_ifgate_b, L1_xattn_outnorm_w)
    x = x + _L1_ffn_ref(_layernorm(x, axis=-1), L1_ffn_router_w, L1_ffn_router_b, L1_ffn_lang_w, L1_ffn_lang_b, L1_ffn_w1, L1_ffn_b1, L1_ffn_w2, L1_ffn_b2)
    x = x + _L2_xattn_ref(_layernorm(x, axis=-1), ctx_1024, mask_BxS2_bk0, L2_xattn_Wq, L2_xattn_bq, L2_xattn_Wk, L2_xattn_bk, L2_xattn_Wv, L2_xattn_bv, L2_xattn_Wo, L2_xattn_bo)
    x = x + _L2_ffn_ref(_layernorm(x, axis=-1), L2_ffn_gate_w, L2_ffn_Wg, L2_ffn_Wu, L2_ffn_Wd, L2_ffn_Sg, L2_ffn_Su, L2_ffn_Sd)
    x = x + _L3_xattn_ref(_layernorm(x, axis=-1), ctx_1024, mask_BxS2_bk0, L3_xattn_q_w, L3_xattn_q_b, L3_xattn_kv_w, L3_xattn_kv_b, L3_xattn_proj_w, L3_xattn_proj_b)
    x = x + _L3_ffn_ref(_layernorm(x, axis=-1), L3_ffn_rw1, L3_ffn_rb1, L3_ffn_rw2, L3_ffn_rb2, L3_ffn_W1, L3_ffn_b1, L3_ffn_W2, L3_ffn_b2)
    return x

_drawn_inputs = setup_inputs


def setup_inputs(seed=0):
    import zlib

    import numpy as np

    out = dict(_drawn_inputs(seed))
    spreads = {'L0_xattn_bq': (0.0, 0.1),
     'L0_xattn_bout': (0.0, 0.1),
     'L1_xattn_outnorm_w': (0.0, 0.1),
     'L1_ffn_router_b': (0.0, 0.1),
     'L1_ffn_lang_b': (0.0, 2.0),
     'L1_ffn_b1': (0.0, 0.1),
     'L1_ffn_b2': (0.0, 0.1),
     'L3_xattn_q_b': (0.0, 0.678),
     'L3_xattn_kv_b': (0.0, 0.1),
     'L3_xattn_proj_b': (0.0, 0.278),
     'L3_ffn_rb1': (0.0, 0.1),
     'L3_ffn_rb2': (0.0, 0.1),
     'L3_ffn_b1': (0.0, 0.291),
     'L3_ffn_b2': (0.0, 0.455)}
    factors = {'L2_xattn_bq': 7.515,
     'L2_xattn_bk': 64.0,
     'L2_ffn_gate_w': 8.0,
     'L2_ffn_Wg': 8.0,
     'L2_ffn_Wu': 8.0,
     'L2_ffn_Wd': 6.859,
     'L2_ffn_Sg': 3.166,
     'L2_ffn_Su': 2.825,
     'L2_ffn_Sd': 3.455}
    for name, (base, spread) in spreads.items():
        noise = np.random.default_rng([zlib.crc32(name.encode()), seed]).standard_normal(out[name].shape)
        drawn = base * np.exp(spread * noise) if base else spread * noise
        out[name] = jnp.asarray(drawn.astype(out[name].dtype))
    for name, factor in factors.items():
        out[name] = (out[name] * factor).astype(out[name].dtype)
    return out
```

```python
from contextlib import ExitStack

import concourse.bass as bass
from concourse import mybir

STAGES = 8

ALU = mybir.AluOpType
ACT = mybir.ActivationFunctionType
F32 = mybir.dt.float32
I32 = mybir.dt.int32
U8 = mybir.dt.uint8
BF16 = mybir.dt.bfloat16
AX = mybir.AxisListType

P = 128
B, S, D = 64, 64, 128
T = B * S
NT = T // P
CH = 512
NC = T // CH
TPC = CH // P
FF = 512
HS = FF // P
LN_EPS = 1e-5
BIG = 3.0e38
NE = 8
RING = 4
YROWS = 2 * T + 80 * P
XROW = 144


class Kernel:

    def __init__(self, nc, ctx, dram):
        self.nc, self.ctx, self.dram, self.sems = nc, ctx, dram, []
        self.x = self.sb("x", [P, NT, D])
        self.xn = self.sb("xn", [P, NT, D])
        self.xnT = self.sb("xnT", [P, T])
        self.ctxT = self.sb("ctxT", [P, T])
        self.ident = self.sb("ident", [P, P])
        self.ones = self.sb("ones", [P, P])
        self.bank = [ctx.enter_context(nc.psum_tensor(f"bank{i}", [P, CH], F32)) for i in range(8)]

    def sb(self, name, shape, dt=F32):
        return self.ctx.enter_context(self.nc.sbuf_tensor(name, shape, dt))

    def sem(self, name):
        self.sems.append(self.nc.alloc_semaphore(name=name))
        return self.sems[-1]

    def end_stage(self):
        self.nc.clear_and_free_semaphores(self.sems)
        self.nc.all_engine_barrier()
        self.sems = []

    def scratch(self, name, shape):
        return self.nc.dram_tensor(name, shape, F32, kind="Internal").ap()


class Steps:

    def __init__(self, eng, sem):
        self.eng, self.sem, self.n = eng, sem, 0

    def __call__(self, ins):
        self.n += 1
        ins.then_inc(self.sem, 1)
        self.eng.wait_ge(self.sem, self.n)


def flat(ap):
    return ap.rearrange("p a b -> p (a b)")


def load_inputs(k):
    nc = k.nc
    loaded, filled = k.sem("inputs_loaded"), k.sem("consts_filled")
    with nc.Block() as block:
        @block.sync
        def _(sp):
            sp.dma_start(k.x[:], k.dram["x"].rearrange("b s d -> (b s) d").rearrange("(j p) d -> p j d", p=P)).then_inc(loaded, 16)
            sp.dma_start(k.ctxT[:], k.dram["ctxT"]).then_inc(loaded, 16)
            sp.wait_ge(loaded, 32)

        @block.gpsimd
        def _(pool):
            nc.gpsimd.memset(k.ones[:], 1.0)
            nc.gpsimd.memset(k.ident[:], 0.0).then_inc(filled, 1)
            pool.wait_ge(filled, 1)
            nc.gpsimd.affine_select(out=k.ident[:], in_=k.ident[:], compare_op=ALU.not_equal, fill=1.0,
                                    base=0, pattern=[[-1, P]], channel_multiplier=1)


def inverse_root(step, nc, root, v, tmp):
    step(nc.vector.reciprocal(root, root))
    step(nc.vector.tensor_tensor(tmp, root, root, ALU.mult))
    step(nc.vector.tensor_tensor(tmp, tmp, v, ALU.mult))
    step(nc.vector.tensor_scalar(tmp, tmp, -0.5, 1.5, ALU.mult, ALU.add))
    step(nc.vector.tensor_tensor(root, root, tmp, ALU.mult))


def layer_norm(k, n):
    nc = k.nc
    with ExitStack() as st:
        stats = st.enter_context(nc.sbuf_tensor(f"ln_stats{n}", [P, NT, 6], F32))
        mv = st.enter_context(nc.sbuf_tensor(f"ln_mv{n}", [P, NT, 2], F32))
        rstd = st.enter_context(nc.sbuf_tensor(f"ln_rstd{n}", [P, NT, 2], F32))
        stats_done, mv_done, var_done = k.sem(f"ln_stats_done{n}"), k.sem(f"ln_mv_done{n}"), k.sem(f"ln_var_done{n}")
        root_done, normed, turned, copied = (k.sem(f"ln_root_done{n}"), k.sem(f"ln_normed{n}"),
                                             k.sem(f"ln_turned{n}"), k.sem(f"ln_copied{n}"))
        with nc.Block() as block:
            @block.vector
            def _(dve):
                for j in range(NT):
                    last = nc.vector.bn_stats(stats[:, j, :], k.x[:, j, :])
                last.then_inc(stats_done, 1)
                dve.wait_ge(stats_done, 1)
                step = Steps(dve, mv_done)
                step(nc.vector.tensor_tensor(mv[:, :, 0], stats[:, :, 1], stats[:, :, 4], ALU.add))
                step(nc.vector.tensor_tensor(mv[:, :, 1], stats[:, :, 1], stats[:, :, 4], ALU.subtract))
                step(nc.vector.tensor_scalar(mv[:, :, 0], mv[:, :, 0], 0.5, None, ALU.mult))
                step(nc.vector.scalar_tensor_tensor(out=mv[:, :, 1], in0=mv[:, :, 1], scalar=0.25, in1=mv[:, :, 1],
                                                    op0=ALU.mult, op1=ALU.mult))
                step(nc.vector.tensor_tensor(rstd[:, :, 0], stats[:, :, 2], stats[:, :, 5], ALU.add))
                step(nc.vector.tensor_scalar(rstd[:, :, 0], rstd[:, :, 0], 1.0 / D, LN_EPS, ALU.mult, ALU.add))
                nc.vector.tensor_tensor(rstd[:, :, 0], rstd[:, :, 0], mv[:, :, 1], ALU.add).then_inc(var_done, 1)
                dve.wait_ge(root_done, 1)
                inverse_root(step, nc, rstd[:, :, 1], rstd[:, :, 0], mv[:, :, 1])
                for j in range(NT):
                    last = nc.vector.tensor_scalar(k.xn[:, j, :], k.x[:, j, :], mv[:, j, 0:1], rstd[:, j, 1:2],
                                                   ALU.subtract, ALU.mult)
                    if j % TPC == TPC - 1:
                        last.then_inc(normed, 1)

            @block.tensor
            def _(pe):
                for g in range(NC):
                    pe.wait_ge(normed, g + 1)
                    if g >= 4:
                        pe.wait_ge(copied, g - 3)
                    for i in range(TPC):
                        last = nc.tensor.transpose(k.bank[g % 4][:, i * P:(i + 1) * P], k.xn[:, g * TPC + i, :], k.ident[:])
                    last.then_inc(turned, 1)

            @block.scalar
            def _(act):
                act.wait_ge(var_done, 1)
                nc.scalar.activation(rstd[:, :, 1], rstd[:, :, 0], ACT.Sqrt).then_inc(root_done, 1)
                for g in range(NC):
                    act.wait_ge(turned, g + 1)
                    nc.scalar.copy(k.xnT[:, g * CH:(g + 1) * CH], k.bank[g % 4][:]).then_inc(copied, 1)


def autocorrelation_attention(k):
    nc = k.nc
    DH, TOP = 8, 11
    with ExitStack() as st:
        def sb(name, shape, dt=F32):
            return st.enter_context(nc.sbuf_tensor(name, shape, dt))
        wq, bq = sb("a0_wq", [P, DH]), sb("a0_bq", [DH, 1])
        wout, bout = sb("a0_wout", [S, 2, D]), sb("a0_bout", [P, D])
        qkT = sb("a0_qkT", [DH, 2, T])
        rows = sb("a0_rows", [P, 2, 4, S])
        gram = sb("a0_gram", [S, 2, S])
        skew = sb("a0_skew", [S, S])
        corr, left, left2 = sb("a0_corr", [P, S]), sb("a0_left", [P, S]), sb("a0_left2", [P, S])
        top, top2 = sb("a0_top", [P, 8]), sb("a0_top2", [P, 8])
        w, ew, sc = sb("a0_w", [P, S]), sb("a0_ew", [P, S]), sb("a0_sc", [P, 4])
        circ = sb("a0_circ", [S, S])
        v = sb("a0_v", [S, 4 * P])
        vx = sb("a0_vx", [S, 2, T])
        wroll = sb("a0_wroll", [S, 2, D])
        d_qk = k.scratch("d_qk", [DH, 2, T])
        d_gram = k.scratch("d_gram", [S * P])
        d_w = k.scratch("d_w", [P * S])
        wl, pj, ev, tod, fromd, gr, gc, sk, co, steps, ex = [k.sem("a0_" + s) for s in (
            "weights_loaded", "projected", "evacuated", "qk_stored", "rows_loaded", "gram_done", "gram_copied",
            "skew_moved", "corr_done", "dve_steps", "exp_done")]
        wst, ci, vt, vc, vxc, wr, wrc, om, xa, pre = [k.sem("a0_" + s) for s in (
            "weights_stored", "circ_loaded", "v_turned", "v_copied", "v_spread", "rolled", "rolled_copied", "out_done", "x_added",
            "bias_added")]

        def spread(e):
            return vx[:, e, :].rearrange("m (b h r) -> m b h r", b=B, h=16)

        def chosen(e):
            one = v[:].rearrange("m (b o r e) -> m b o r e", b=B, o=1, e=2)[:, :, :, :, e]
            return one.broadcast_to((S, B, 16, 4))

        with nc.Block() as block:
            @block.sync
            def _(sp):
                sp.dma_start(wq[:], k.dram["L0_xattn_Wq"]).then_inc(wl, 16)
                sp.dma_start(bq[:], k.dram["L0_xattn_bq"].rearrange("(d o) -> d o", o=1)).then_inc(wl, 16)
                sp.dma_start(wout[:], k.dram["L0_xattn_Wout"].rearrange("(e l) n -> l e n", e=2)).then_inc(wl, 16)
                sp.dma_start(bout[:], k.dram["L0_xattn_bout"].partition_broadcast(P)).then_inc(wl, 16)
                sp.wait_ge(ev, 2 * NC)
                sp.dma_start(d_qk, qkT[:]).then_inc(tod, 16)
                sp.wait_ge(tod, 16)
                for d in range(DH):
                    for i in range(2):
                        sp.dma_start(rows[d::DH, i], d_qk[d, i].rearrange("(c b m) -> b c m", c=4, b=16)).then_inc(fromd, 16)
                sp.wait_ge(gc, 2)
                sp.dma_start(d_gram.rearrange("(n m) -> n m", n=S), gram[:].rearrange("n a m -> n (a m)")).then_inc(sk, 16)
                sp.wait_ge(sk, 16)
                sp.dma_start(skew[:], bass.AP(d_gram.tensor, 0, [[P + 1, S], [1, S]])).then_inc(sk, 16)
                sp.wait_ge(steps, 11)
                sp.dma_start(d_w.rearrange("(p m) -> p m", p=P), w[:]).then_inc(wst, 16)
                sp.wait_ge(wst, 16)
                sp.dma_start(circ[:], bass.AP(d_w.tensor, 0, [[P - 1, S], [1, S]])).then_inc(ci, 16)

            @block.gpsimd
            def _(pool):
                pool.wait_ge(wl, 64)
                nc.gpsimd.tensor_tensor(k.x[:], k.x[:], bout[:].rearrange("p (o d) -> p o d", o=1).broadcast_to((P, NT, D)),
                                        ALU.add).then_inc(pre, 1)
                pool.wait_ge(vc, 1)
                nc.gpsimd.tensor_copy(spread(1), chosen(1)).then_inc(vxc, 1)

            @block.tensor
            def _(pe):
                pe.wait_ge(wl, 64)
                for c in range(NC):
                    for i, src in enumerate((k.xnT, k.ctxT)):
                        n = 2 * c + i
                        if n >= 4:
                            pe.wait_ge(ev, n - 3)
                        nc.tensor.matmul(k.bank[n % 4][0:DH, :], wq[:], src[:, c * CH:(c + 1) * CH],
                                         start=True, stop=True).then_inc(pj, 1)
                pe.wait_ge(fromd, 32 * DH)
                for c in range(4):
                    last = nc.tensor.matmul(k.bank[4][0:S, 0:S], rows[:, 1, c, :], rows[:, 0, c, :], start=c == 0, stop=c == 3)
                last.then_inc(gr, 1)
                for c in range(4):
                    last = nc.tensor.transpose(k.bank[5][0:S, c * P:(c + 1) * P], rows[:, 1, c, :], k.ident[:])
                last.then_inc(vt, 1)
                pe.wait_ge(sk, 32)
                nc.tensor.matmul(k.bank[6][:, 0:S], k.ones[0:S, :], skew[:], start=True, stop=True).then_inc(co, 1)
                pe.wait_ge(ci, 16)
                for e in range(2):
                    last = nc.tensor.matmul(k.bank[7][0:S, e * D:(e + 1) * D], circ[:], wout[:, e, :], start=True, stop=True)
                last.then_inc(wr, 1)
                pe.wait_ge(wrc, 1)
                pe.wait_ge(vxc, 2)
                for g in range(NC):
                    if g >= 4:
                        pe.wait_ge(xa, g - 3)
                    for i in range(TPC):
                        j = g * TPC + i
                        for e in range(2):
                            last = nc.tensor.matmul(k.bank[g % 4][:, i * D:(i + 1) * D], vx[:, e, j * P:(j + 1) * P], wroll[:, e, :], start=e == 0, stop=e == 1)
                    last.then_inc(om, 1)

            @block.scalar
            def _(act):
                act.wait_ge(wl, 64)
                for n in range(2 * NC):
                    act.wait_ge(pj, n + 1)
                    c, i = n // 2, n % 2
                    nc.scalar.activation(qkT[:, i, c * CH:(c + 1) * CH], k.bank[n % 4][0:DH, :], ACT.Identity, bias=bq[:]).then_inc(ev, 1)
                act.wait_ge(vt, 1)
                nc.scalar.copy(v[:], k.bank[5][0:S, :]).then_inc(vc, 1)
                act.wait_ge(steps, 8)
                nc.scalar.activation(ew[:], corr[:], ACT.Exp, bias=sc[:, 0:1]).then_inc(ex, 1)
                act.wait_ge(wr, 1)
                nc.scalar.copy(wroll[:].rearrange("m e n -> m (e n)"), k.bank[7][0:S, 0:2 * D]).then_inc(wrc, 1)

            @block.vector
            def _(dve):
                step = Steps(dve, steps)
                dve.wait_ge(vc, 1)
                nc.vector.tensor_copy(spread(0), chosen(0)).then_inc(vxc, 1)
                dve.wait_ge(gr, 1)
                for i in range(2):
                    nc.vector.tensor_copy(gram[:, i, :], k.bank[4][0:S, 0:S]).then_inc(gc, 1)
                dve.wait_ge(co, 1)
                step(nc.vector.tensor_scalar(corr[:], k.bank[6][:, 0:S], 1.0 / (B * DH), None, ALU.mult))
                step(nc.vector.max(top[:], corr[:]))
                step(nc.vector.match_replace(left[:], top[:], corr[:], -BIG))
                step(nc.vector.max(top2[:], left[:]))
                step(nc.vector.memset(top2[:, TOP - 8:], -BIG))
                step(nc.vector.match_replace(left2[:], top2[:], left[:], -BIG))
                step(nc.vector.tensor_scalar(left[:], left2[:], -0.5 * BIG, None, ALU.is_le))
                step(nc.vector.tensor_scalar(sc[:, 0:1], top[:, 0:1], -1.0, None, ALU.mult))
                dve.wait_ge(ex, 1)
                step(nc.vector.tensor_tensor_reduce(out=w[:], in0=ew[:], in1=left[:], scale=1.0, scalar=0.0,
                                                    op0=ALU.mult, op1=ALU.add, accum_out=sc[:, 1:2]))
                step(nc.vector.reciprocal(sc[:, 2:3], sc[:, 1:2]))
                step(nc.vector.tensor_scalar(w[:], w[:], sc[:, 2:3], None, ALU.mult))
                dve.wait_ge(pre, 1)
                for g in range(NC):
                    dve.wait_ge(om, g + 1)
                    xs = flat(k.x[:, g * TPC:(g + 1) * TPC, :])
                    nc.vector.tensor_tensor(xs, k.bank[g % 4][:], xs, ALU.add).then_inc(xa, 1)


def wait(eng, sem, value):
    if not isinstance(value, int) or value > 0:
        eng.wait_ge(sem, value)


def turns(eng, n, body):
    body(0)
    with eng.Fori(1, n) as i:
        body(i)


def make_tables(k):
    nc = k.nc
    k.tri = k.sb("tri", [P, P])
    k.iota = k.sb("iota", [P, P], BF16)
    k.iota_f = k.sb("iota_f", [P, P])
    k.pcol = k.sb("pcol", [P, 3])
    k.jval = k.sb("jval", [P, 2, NT])
    k.rev = k.sb("rev", [P, NE])
    k.zeros = k.sb("zeros", [P, XROW])
    made = k.sem("tables_made")
    with nc.Block() as block:
        @block.gpsimd
        def _(pool):
            nc.gpsimd.memset(k.zeros[:], 0.0)
            nc.gpsimd.memset(k.tri[:], 1.0).then_inc(made, 1)
            nc.gpsimd.iota(k.iota[:], [[1, P]], base=0, channel_multiplier=0, allow_small_or_imprecise_dtypes=True)
            nc.gpsimd.iota(k.iota_f[:], [[1, P]], base=0, channel_multiplier=0, allow_small_or_imprecise_dtypes=True)
            nc.gpsimd.iota(k.pcol[:, 0:1], [[0, 1]], base=1, channel_multiplier=1, allow_small_or_imprecise_dtypes=True)
            nc.gpsimd.iota(k.pcol[:, 1:2], [[0, 1]], base=2 * T, channel_multiplier=1, allow_small_or_imprecise_dtypes=True)
            nc.gpsimd.iota(k.pcol[:, 2:3], [[0, 1]], base=T, channel_multiplier=1, allow_small_or_imprecise_dtypes=True)
            nc.gpsimd.iota(k.jval[:], [[NT, 2], [1, NT]], base=0, channel_multiplier=0, allow_small_or_imprecise_dtypes=True)
            nc.gpsimd.iota(k.rev[:], [[-1, NE]], base=NE, channel_multiplier=0, allow_small_or_imprecise_dtypes=True)
            pool.wait_ge(made, 1)
            nc.gpsimd.affine_select(out=k.tri[:], in_=k.tri[:], compare_op=ALU.is_gt, fill=0.0,
                                    base=0, pattern=[[1, P]], channel_multiplier=-1)


def bc(ap, shape, axis):
    names = list("abcd"[:len(ap.shape)])
    if axis == len(names):
        src = " ".join(names[:-1]) + f" ({names[-1]} o)"
    else:
        src = " ".join(names[:axis]) + f" (o {names[axis]}) " + " ".join(names[axis + 1:])
    out = names[:axis] + ["o"] + names[axis:]
    return ap.rearrange(f"{src} -> {' '.join(out)}", o=1).broadcast_to(shape)


class Moe:

    def __init__(self, k, tag, choices, w1, w2, act, b1=None, b2=None):
        self.k, self.tag, self.choices, self.act = k, tag, choices, act
        self.w1, self.w2, self.b1, self.b2 = w1, w2, b1, b2
        tiles = choices * NT + NE - 1
        self.tiles = -(-tiles // RING) * RING
        self.cols = self.tiles + RING


def route(k, st, m, weights):
    nc, tag = k.nc, m.tag

    def sb(name, shape, dt=F32):
        return st.enter_context(nc.sbuf_tensor(f"{tag}_{name}", shape, dt))
    SH = (P, NT, NE)
    lg = m.lg
    m.gate = sb("gate", [P, 2, NT])
    m.src = sb("src", [P, m.cols], I32)
    m.dst = sb("dst", [P, m.cols], I32)
    m.expert = sb("expert", [1, m.cols], I32)
    with ExitStack() as tmp:
        def tb(name, shape, dt=F32):
            return tmp.enter_context(nc.sbuf_tensor(f"{tag}_{name}", shape, dt))
        t1, t2, oh1, oh2, any_ = [tb(n, [P, NT, NE]) for n in ("t1", "t2", "oh1", "oh2", "any")]
        mx = tb("mx", [P, 4, NT])
        cnt, cum, exc, slotv = [tb(n, [P, NE, NT]) for n in ("cnt", "cum", "exc", "slotv")]
        small = tb("small", [P, 6, NE])
        smalli = tb("smalli", [P, NE], I32)
        slot, sloti, sloti2 = tb("slot", [P, 2, NT]), tb("sloti", [P, 2, NT], I32), tb("sloti2", [P, 2, NT], I32)
        ri, ii = tb("ri", [P, 2, NT]), tb("ii", [P, 2, NT])
        cmp_ = tb("cmp", [P, m.cols, NE])
        ef = tb("ef", [P, m.cols])
        ones_r = tb("ones_r", [P, NE * NT])
        ohr = tb("ohr", [P, 4, P], BF16)
        ohi = tb("ohi", [P, 4, 2, m.cols], BF16)
        jj, pp, f1, f2 = [tb(n, [P, m.cols]) for n in ("jj", "pp", "f1", "f2")]
        steps, exd, exc_done, rk, oh, inv = [k.sem(f"{tag}_{s}") for s in (
            "dve_steps", "exp_done", "any_ready", "ranked", "onehots", "inverted")]
        xst, wl, one_used = [k.sem(f"{tag}_{s}") for s in ("xn_stored", "weights_loaded", "onehots_used")]
        m.weights_loaded = wl
        count = {}
        with nc.Block() as block:
            @block.sync
            def _(sp):
                sp.dma_start(k.d_xn[0:T, :].rearrange("(j p) d -> p j d", p=P), k.xn[:]).then_inc(xst, 16)
                for dst, src in weights:
                    sp.dma_start(dst, src).then_inc(wl, 16)
                sp.wait_ge(xst, 16)
                sp.wait_ge(wl, 16 * len(weights))

            @block.vector
            def _(dve):
                step = Steps(dve, steps)
                TT, TS, RED = nc.vector.tensor_tensor, nc.vector.tensor_scalar, nc.vector.tensor_reduce

                def pick(src, best, onehot):
                    step(RED(best, src, AX.X, ALU.max))
                    step(TT(t1[:], src, bc(best, SH, 2), ALU.is_equal))
                    step(TT(t1[:], t1[:], bc(k.rev[:], SH, 1), ALU.mult))
                    step(RED(mx[:, 2, :], t1[:], AX.X, ALU.max))
                    step(TT(onehot[:], t1[:], bc(mx[:, 2, :], SH, 2), ALU.is_equal))
                pick(lg[:], mx[:, 0, :], oh1)
                step(nc.vector.scalar_tensor_tensor(out=flat(t2[:]), in0=flat(oh1[:]), scalar=-BIG, in1=flat(lg[:]),
                                                    op0=ALU.mult, op1=ALU.add))
                pick(t2[:], mx[:, 1, :], oh2)
                if m.choices == 2:
                    step(TT(any_[:], oh1[:], oh2[:], ALU.add))
                else:
                    step(nc.vector.tensor_copy(any_[:], oh1[:]))
                step(TT(mx[:, 3, :], mx[:, 1, :], mx[:, 0, :], ALU.subtract))
                count["any"] = step.n
                dve.wait_ge(exd, 1)
                step(TS(m.gate[:, 0, :], m.gate[:, 1, :], 1.0, None, ALU.add))
                step(nc.vector.reciprocal(m.gate[:, 0, :], m.gate[:, 0, :]))
                step(TT(m.gate[:, 1, :], m.gate[:, 1, :], m.gate[:, 0, :], ALU.mult))
                step(nc.vector.memset(ones_r[:], 1.0))
                dve.wait_ge(rk, 1)
                step(nc.vector.tensor_copy(cnt[:], k.bank[0][:, NE * NT:].rearrange("p (j e) -> p e j", e=NE)))
                step(nc.vector.tensor_tensor_scan(flat(cum[:]), ones_r[:], flat(cnt[:]), 0.0, ALU.mult, ALU.add))
                step(TT(exc[:], cum[:], cnt[:], ALU.subtract))
                start, n_e, tiles_e, cumt, base = [small[:, i, :] for i in range(5)]
                step(TT(n_e, cum[:, :, NT - 1], exc[:, :, 0], ALU.subtract))
                step(TS(smalli[:], n_e, float(P - 1), None, ALU.add))
                step(TS(smalli[:], smalli[:], 7, None, ALU.arith_shift_right))
                step(nc.vector.tensor_copy(tiles_e, smalli[:]))
                step(nc.vector.tensor_tensor_scan(cumt, ones_r[:, 0:NE], tiles_e, 0.0, ALU.mult, ALU.add))
                step(TT(base, cumt, tiles_e, ALU.subtract))
                step(TS(base, base, float(P), None, ALU.mult))
                step(TT(base, base, exc[:, :, 0], ALU.subtract))
                step(TT(exc[:], exc[:], bc(base, (P, NE, NT), 2), ALU.add))
                step(TT(slotv[:], k.bank[0][:, 0:NE * NT].rearrange("p (j e) -> p e j", e=NE), exc[:], ALU.add))
                for c, hot in enumerate((oh1, oh2)[:m.choices]):
                    step(TT(t1[:], hot[:], slotv[:].rearrange("p e j -> p j e"), ALU.mult))
                    step(RED(slot[:, c, :], t1[:], AX.X, ALU.add))
                n = m.choices
                step(nc.vector.tensor_copy(sloti[:, 0:n], slot[:, 0:n]))
                step(TS(sloti2[:, 0:n], sloti[:, 0:n], 7, None, ALU.arith_shift_right))
                step(TS(sloti[:, 0:n], sloti[:, 0:n], P - 1, None, ALU.bitwise_and))
                step(nc.vector.tensor_copy(ii[:, 0:n], sloti2[:, 0:n]))
                step(nc.vector.tensor_copy(ri[:, 0:n], sloti[:, 0:n]))
                fri, fii, fjv = [a[:].rearrange("p a b -> p (a b)") for a in (ri, ii, k.jval)]

                def one_hots(i):
                    wait(dve, one_used, i)
                    for u in range(4):
                        at = bass.ds(i * 4 + u, 1)
                        TS(ohr[:, u, :], k.iota[:], fri[:, at], None, ALU.is_equal)
                        TS(ohi[:, u, 0, :], k.iota[:, 0:m.cols], fii[:, at], fjv[:, at], ALU.is_equal, ALU.mult)
                        last = TS(ohi[:, u, 1, :], k.iota[:, 0:m.cols], fii[:, at], k.pcol[:, 0:1], ALU.is_equal, ALU.mult)
                    last.then_inc(oh, 1)
                turns(dve, NT * n // 4, one_hots)
                step(TT(cmp_[:], bc(k.iota_f[:, 0:m.cols], (P, m.cols, NE), 2), bc(cumt, (P, m.cols, NE), 1), ALU.is_ge))
                step(RED(ef[:], cmp_[:], AX.X, ALU.add))
                step(TS(m.expert[:], ef[0:1, :], float(NE - 1), None, ALU.min))
                dve.wait_ge(inv, 1)
                step(nc.vector.tensor_copy(jj[:], k.bank[1][:, 0:m.cols]))
                step(nc.vector.tensor_copy(pp[:], k.bank[1][:, m.cols:2 * m.cols]))
                step(TS(f1[:], pp[:], 0.0, None, ALU.is_equal))
                step(TS(f2[:], pp[:], 0.0, -1.0, ALU.is_gt, ALU.mult))
                step(TT(pp[:], pp[:], f2[:], ALU.add))
                step(nc.vector.scalar_tensor_tensor(out=pp[:], in0=jj[:], scalar=float(P), in1=pp[:], op0=ALU.mult, op1=ALU.add))
                step(TS(jj[:], k.iota_f[:, 0:m.cols], float(P), k.pcol[:, 1:2], ALU.mult, ALU.add))
                step(TT(jj[:], jj[:], f1[:], ALU.mult))
                step(TT(m.dst[:], jj[:], pp[:], ALU.add))
                step(TS(f2[:], pp[:], float(T), -float(T), ALU.is_ge, ALU.mult))
                step(TT(pp[:], pp[:], f2[:], ALU.add))
                step(TS(f1[:], f1[:], k.pcol[:, 2:3], None, ALU.mult))
                step(TT(m.src[:], pp[:], f1[:], ALU.add))

            @block.scalar
            def _(act):
                act.wait_ge(steps, count_any(m))
                nc.scalar.activation(m.gate[:, 1, :], mx[:, 3, :], ACT.Exp).then_inc(exd, 1)

            @block.tensor
            def _(pe):
                pe.wait_ge(steps, count_any(m))
                nc.tensor.matmul(k.bank[0][:, 0:NE * NT], k.tri[:], flat(any_[:]), start=True, stop=True)
                nc.tensor.matmul(k.bank[0][:, NE * NT:], k.ones[:], flat(any_[:]), start=True, stop=True).then_inc(rk, 1)
                G = NT * m.choices // 4
                pe.wait_ge(oh, 1)

                def invert(u, start, stop):
                    return nc.tensor.matmul(k.bank[1][:, 0:2 * m.cols], ohr[:, u, :], ohi[:, u].rearrange("p a b -> p (a b)"),
                                            start=start, stop=stop)
                for u in range(4):
                    last = invert(u, u == 0, False)
                last.then_inc(one_used, 1)
                with pe.Fori(1, G - 1) as i:
                    pe.wait_ge(oh, i + 1)
                    for u in range(4):
                        last = invert(u, False, False)
                    last.then_inc(one_used, 1)
                pe.wait_ge(oh, G)
                for u in range(4):
                    last = invert(u, False, u == 3)
                last.then_inc(inv, 1)


def count_any(m):
    return 13


def experts(k, m):
    nc, tag = k.nc, m.tag
    N = m.tiles
    BT, BH, BG, BY = k.bank[0], k.bank[1], k.bank[2], k.bank[3]
    with ExitStack() as st:
        def sb(name, shape, dt=F32):
            return st.enter_context(nc.sbuf_tensor(f"{tag}_{name}", shape, dt))
        xs = sb("xs", [P, RING, D])
        xsT = sb("xsT", [P, P])
        hpre = sb("hpre", [P, FF])
        hT = sb("hT", [P, HS, P])
        y = sb("y", [P, RING, D])
        gathered = [k.sem(f"{tag}_gathered{u}") for u in range(RING)]
        scattered = [k.sem(f"{tag}_scattered{u}") for u in range(RING)]
        x_turned, x_copied, up, biased, h_turned, activated, down, y_ready = [k.sem(f"{tag}_{s}") for s in (
            "x_turned", "x_copied", "up_done", "biased", "h_turned", "activated", "down_done", "y_ready")]
        with nc.Block() as block:
            @block.gpsimd
            def _(pool):
                def gather(n):
                    nc.gpsimd.indirect_dma_start(xs[:, n % RING, :], None, k.d_xn,
                                                 bass.IndirectOffsetOnAxis(m.src[:, n:n + 1], 0)).then_inc(gathered[n % RING], 16)
                for n in range(RING):
                    gather(n)
                for n in range(N):
                    pool.wait_ge(y_ready, n + 1)
                    nc.gpsimd.indirect_dma_start(k.d_y, bass.IndirectOffsetOnAxis(m.dst[:, n:n + 1], 0),
                                                 y[:, n % RING, :], None).then_inc(scattered[n % RING], 16)
                    pool.wait_ge(x_turned, n + 1)
                    gather(n + RING)
                for u in range(RING):
                    pool.wait_ge(scattered[u], 16 * (N // RING))
                    pool.wait_ge(gathered[u], 16 * (N // RING + 1))

            @block.tensor
            def _(pe):
                def turn_x(n, u):
                    wait(pe, x_copied, n)
                    nc.tensor.transpose(BT[:, 0:P], xs[:, u, :], k.ident[:]).then_inc(x_turned, 1)

                def expert_of(n):
                    return pe.value_load(m.expert[0:1, bass.ds(n, 1)], min_val=0, max_val=NE - 1)

                def up_proj(n, e):
                    pe.wait_ge(x_copied, n + 1)
                    wait(pe, biased, n)
                    nc.tensor.matmul(BH[:], xsT[:], m.w1[:, bass.ds(e * FF, FF)], start=True, stop=True).then_inc(up, 1)

                def turn_h(n):
                    pe.wait_ge(biased, n + 1)
                    wait(pe, activated, n)
                    for s in range(HS):
                        last = nc.tensor.transpose(BG[:, s * P:(s + 1) * P], hpre[:, s * P:(s + 1) * P], k.ident[:])
                    last.then_inc(h_turned, 1)

                def down_proj(n, e):
                    pe.wait_ge(activated, n + 1)
                    wait(pe, y_ready, n)
                    for s in range(HS):
                        last = nc.tensor.matmul(BY[:, 0:D], hT[:, s, :], m.w2[:, bass.ds(e * FF + s * D, D)],
                                                start=s == 0, stop=s == HS - 1)
                    last.then_inc(down, 1)
                pe.wait_ge(gathered[0], 16)
                turn_x(0, 0)
                up_proj(0, expert_of(0))
                pe.wait_ge(gathered[1], 16)
                turn_x(1, 1)
                turn_h(0)

                def body(i):
                    es = [expert_of(RING * i), expert_of(RING * i + 1)]
                    for u in range(RING):
                        n = RING * i + u
                        up_proj(n + 1, es[u + 1])
                        if u + 2 <= RING:
                            es.append(expert_of(n + 2))
                        down_proj(n, es[u])
                        v = (u + 2) % RING
                        pe.wait_ge(gathered[v], 16 * (i + 1) + (16 if u + 2 >= RING else 0))
                        turn_x(n + 2, v)
                        turn_h(n + 1)
                turns(pe, N // RING, body)

            @block.scalar
            def _(act):
                def copy_x(n):
                    act.wait_ge(x_turned, n + 1)
                    wait(act, up, n)
                    nc.scalar.copy(xsT[:], BT[:, 0:P]).then_inc(x_copied, 1)

                def activate(n):
                    act.wait_ge(h_turned, n + 1)
                    wait(act, down, n)
                    nc.scalar.activation(flat(hT[:]), BG[:], m.act).then_inc(activated, 1)
                copy_x(0)
                copy_x(1)
                activate(0)
                with act.Fori(0, N) as n:
                    copy_x(n + 2)
                    activate(n + 1)

            @block.vector
            def _(dve):
                def expert_of(n):
                    return dve.value_load(m.expert[0:1, bass.ds(n, 1)], min_val=0, max_val=NE - 1) if m.b1 is not None else None

                def bias(n, e):
                    dve.wait_ge(up, n + 1)
                    wait(dve, h_turned, n)
                    if m.b1 is None:
                        nc.vector.tensor_copy(hpre[:], BH[:]).then_inc(biased, 1)
                    else:
                        nc.vector.tensor_tensor(hpre[:], BH[:], m.b1[:, bass.ds(e * FF, FF)], ALU.add).then_inc(biased, 1)
                bias(0, expert_of(0))

                def body(i):
                    es = [expert_of(RING * i), expert_of(RING * i + 1)]
                    for u in range(RING):
                        n = RING * i + u
                        bias(n + 1, es[u + 1])
                        if u + 2 <= RING:
                            es.append(expert_of(n + 2))
                        e = es[u]
                        dve.wait_ge(down, n + 1)
                        wait(dve, scattered[u], 16 * i)
                        if m.b2 is None:
                            nc.vector.tensor_copy(y[:, u, :], BY[:, 0:D]).then_inc(y_ready, 1)
                        else:
                            nc.vector.tensor_tensor(y[:, u, :], BY[:, 0:D], m.b2[:, bass.ds(e * D, D)], ALU.add).then_inc(y_ready, 1)
                turns(dve, N // RING, body)


def combine(k, m):
    nc, tag = k.nc, m.tag
    PARTS, TP = 4, NT // 4
    with ExitStack() as st:
        y = st.enter_context(nc.sbuf_tensor(f"{tag}_yback", [P, 2, TP, D], F32))
        back = [k.sem(f"{tag}_y_back{u}") for u in range(2)]
        added = k.sem(f"{tag}_y_added")
        parts = [(c, q) for q in range(PARTS) for c in range(m.choices)]
        with nc.Block() as block:
            @block.sync
            def _(sp):
                for n, (c, q) in enumerate(parts):
                    if n >= 2:
                        sp.wait_ge(added, TP * (n - 1))
                    rows = k.d_y[c * T + q * TP * P:c * T + (q + 1) * TP * P, :]
                    sp.dma_start(y[:, n % 2], rows.rearrange("(j p) d -> p j d", p=P)).then_inc(back[n % 2], 16)

            @block.vector
            def _(dve):
                for n, (c, q) in enumerate(parts):
                    dve.wait_ge(back[n % 2], 16 * (n // 2 + 1))
                    if n >= 1:
                        dve.wait_ge(added, TP * n)
                    for t in range(TP):
                        j = q * TP + t
                        nc.vector.scalar_tensor_tensor(out=k.x[:, j, :], in0=y[:, n % 2, t, :], scalar=m.gate[:, c, j:j + 1],
                                                       in1=k.x[:, j, :], op0=ALU.mult, op1=ALU.add).then_inc(added, 1)


def token_logits(k, tag, lg, w, cols, bias=None):
    nc = k.nc
    done, out = k.sem(f"{tag}_logits_done"), k.sem(f"{tag}_logits_copied")
    with nc.Block() as block:
        @block.tensor
        def _(pe):
            for j in range(NT):
                last = nc.tensor.matmul(k.bank[7][:, j * cols:(j + 1) * cols], k.xnT[:, j * P:(j + 1) * P], w, start=True, stop=True)
            last.then_inc(done, 1)

        @block.vector
        def _(dve):
            dve.wait_ge(done, 1)
            ps = k.bank[7][:, 0:NT * cols].rearrange("p (j c) -> p j c", c=cols)
            if bias is None:
                nc.vector.tensor_copy(lg, ps)
            else:
                nc.vector.tensor_tensor(lg, ps, bc(bias, (P, NT, cols), 1), ALU.add)


def moe_top1(k):
    nc = k.nc
    with ExitStack() as st:
        def sb(name, shape, dt=F32):
            return st.enter_context(nc.sbuf_tensor(name, shape, dt))
        w1, w2 = sb("f0_w1", [P, NE * FF]), sb("f0_w2", [P, NE * FF])
        m = Moe(k, "f0", 1, w1, w2, ACT.Gelu)
        wr = sb("f0_wr", [P, NE])
        m.lg = sb("f0_lg", [P, NT, NE])
        got = k.sem("f0_router_loaded")
        with nc.Block() as block:
            @block.sync
            def _(sp):
                sp.dma_start(wr[:], k.dram["L0_ffn_Wr"]).then_inc(got, 16)
                sp.wait_ge(got, 16)
        token_logits(k, "f0", m.lg[:], wr[:], NE)
        route(k, st, m, expert_weights(k, w1, w2, "L0_ffn_W1", "L0_ffn_W2"))
        experts(k, m)
        combine(k, m)


def make_attention_tables(k):
    nc = k.nc
    k.head16 = k.sb("head16", [P, 16])
    k.head8 = k.sb("head8", [P, 8])
    k.cumtri = k.sb("cumtri", [P, P])
    k.causal = k.sb("causal", [P, S])
    made = k.sem("attention_tables_made")
    with nc.Block() as block:
        @block.gpsimd
        def _(pool):
            g = nc.gpsimd
            n = 0

            def step(ins):
                nonlocal n
                n += 1
                ins.then_inc(made, 1)
                pool.wait_ge(made, n)
            for table, heads in ((k.head16, 16), (k.head8, 8)):
                w = P // heads
                step(g.memset(table[:], 1.0))
                step(g.affine_select(out=table[:], in_=table[:], compare_op=ALU.is_ge, fill=0.0, base=0,
                                     pattern=[[-w, heads]], channel_multiplier=1))
                step(g.affine_select(out=table[:], in_=table[:], compare_op=ALU.is_ge, fill=0.0, base=w - 1,
                                     pattern=[[w, heads]], channel_multiplier=-1))
            step(g.memset(k.cumtri[:], 1.0))
            step(g.affine_select(out=k.cumtri[:], in_=k.cumtri[:], compare_op=ALU.is_ge, fill=0.0, base=0,
                                 pattern=[[1, P]], channel_multiplier=-1))
            step(g.memset(k.cumtri[0:S, S:P], 0.0))
            step(g.memset(k.causal[:], 0.0))
            for h in range(2):
                half = k.causal[h * S:(h + 1) * S, :]
                step(g.affine_select(out=half, in_=half, compare_op=ALU.is_ge, fill=-BIG, base=0,
                                     pattern=[[1, S]], channel_multiplier=-1))


def mlstm(k):
    nc = k.nc
    NH, DH, CAP = 8, 16, 15.0
    VW = 2 * (DH + 1)
    H2 = NH // 2
    with ExitStack() as st:
        def sb(name, shape, dt=F32):
            return st.enter_context(nc.sbuf_tensor(f"a1_{name}", shape, dt))

        def sem(name):
            return k.sem(f"a1_{name}")
        vb = sb("vb", [P, B * H2 * VW + P])
        vb4 = vb[:, 0:B * H2 * VW].rearrange("p (b q w) -> p b q w", b=B, q=H2)
        a_b = sb("a_b", [P, B, H2])
        lfc, a, m_t = sb("lfc", [P, NT, NH]), sb("a", [P, NT, NH]), sb("m_t", [P, NT, NH])
        gain = sb("gain", [P, D])
        hout = sb("hout", [P, NT, NH, DH + 1])
        d_m = k.scratch("d_m", [B, 2, H2, S])

        with ExitStack() as tmp:
            def tb(name, shape, dt=F32):
                return tmp.enter_context(nc.sbuf_tensor(f"a1_{name}", shape, dt))
            w3 = tb("w3", [P, 3, 2 * NH])
            gbias = tb("gbias", [P, 2 * NH])
            v2 = tb("v2", [P, B // 2, D])
            pre = tb("pre", [P, NT, 2 * NH])
            logf = tb("logf", [P, NT, NH])
            aT2 = tb("aT2", [P, 2, 2, 2, S])
            mT = tb("mT", [P, 2, 2, S])
            wl, vl, spread, steps, gates, capped, lnd, cums, aT_done, aT_back, mT_done, stored, padded = [sem(s) for s in (
                "weights_loaded", "v_loaded", "v_spread", "dve_steps", "gates_done", "act_steps", "log_done",
                "summed", "a_turned", "a_turned_back", "m_turned", "m_stored", "padded")]
            with nc.Block() as block:
                @block.sync
                def _(sp):
                    sp.dma_start(w3[:], k.dram["ifgate_wT"].rearrange("(i d) g -> d i g", i=3)).then_inc(wl, 16)
                    sp.dma_start(gbias[:], k.dram["L1_xattn_ifgate_b"].partition_broadcast(P)).then_inc(wl, 16)
                    sp.dma_start(gain[:], k.dram["L1_xattn_outnorm_w"].partition_broadcast(P)).then_inc(wl, 16)
                    for q in range(2):
                        if q == 1:
                            sp.wait_ge(spread, 2)
                        for h in range(2):
                            sp.dma_start(v2[h * S:(h + 1) * S], k.dram["ctx_1024"][q * B // 2:(q + 1) * B // 2].rearrange(
                                "b s d -> s b d")).then_inc(vl, 16)
                    sp.wait_ge(steps, 13)
                    for h in range(NH):
                        for half in range(2):
                            sp.dma_start(d_m[half * 32:(half + 1) * 32, h % 2, h // 2, :].rearrange("(j b) t -> j b t", b=2),
                                         mT[h::NH, half]).then_inc(stored, 16)
                    sp.wait_ge(stored, 16 * NH * 2)

                @block.gpsimd
                def _(pool):
                    nc.gpsimd.memset(vb[:, B * H2 * VW:], 0.0).then_inc(padded, 1)
                    pool.wait_ge(padded, 1)
                    for h in range(2):
                        nc.gpsimd.memset(vb4[h * S:(h + 1) * S, :, :, (1 - h) * (DH + 1):(2 - h) * (DH + 1)], 0.0)
                        nc.gpsimd.memset(vb4[h * S:(h + 1) * S, :, :, h * (DH + 1) + DH:h * (DH + 1) + DH + 1], 1.0)
                    for q in range(2):
                        pool.wait_ge(vl, 32 * (q + 1))
                        for h in range(2):
                            nc.gpsimd.tensor_copy(
                                vb4[h * S:(h + 1) * S, q * 32:(q + 1) * 32, :, h * (DH + 1):h * (DH + 1) + DH],
                                v2[h * S:(h + 1) * S].rearrange("s b (p t d) -> s b p t d", t=2, d=DH)[:, :, :, h, :]).then_inc(spread, 1)

                @block.tensor
                def _(pe):
                    pe.wait_ge(steps, 1)
                    for j in range(NT):
                        out = k.bank[0][:, j * 16:(j + 1) * 16]
                        nc.tensor.matmul(out, k.xnT[:, j * P:(j + 1) * P], w3[:, 0, :], start=True, stop=False)
                        last = nc.tensor.matmul(out, k.ctxT[:, j * P:(j + 1) * P], w3[:, 1, :], start=False, stop=True)
                    last.then_inc(gates, 1)
                    pe.wait_ge(steps, 4)
                    nc.tensor.matmul(k.bank[1][:, 0:NT * NH], k.cumtri[:], flat(logf[:]), start=True, stop=True).then_inc(cums, 1)
                    pe.wait_ge(steps, 6)
                    for half in range(2):
                        last = nc.tensor.transpose(k.bank[2][:, half * P:(half + 1) * P], flat(a[:])[:, half * P:(half + 1) * P], k.ident[:])
                    last.then_inc(aT_done, 1)
                    pe.wait_ge(steps, 8)
                    for n in range(4):
                        last = nc.tensor.transpose(k.bank[3][:, n * P:(n + 1) * P],
                                                   aT2[:, n // 2, n % 2].rearrange("p c s -> p (c s)"), k.ident[:])
                    last.then_inc(aT_back, 1)
                    pe.wait_ge(steps, 13)
                    for half in range(2):
                        last = nc.tensor.transpose(k.bank[4][:, half * P:(half + 1) * P], mT[:, half].rearrange("p b t -> p (b t)"), k.ident[:])
                    last.then_inc(mT_done, 1)

                @block.scalar
                def _(act):
                    act.wait_ge(steps, 2)
                    nc.scalar.activation(pre[:], pre[:], ACT.Tanh, scale=1.0 / CAP).then_inc(capped, 1)
                    act.wait_ge(capped, 1)
                    nc.scalar.activation(logf[:], pre[:, :, NH:], ACT.Exp, scale=-CAP).then_inc(capped, 1)
                    act.wait_ge(steps, 3)
                    nc.scalar.activation(logf[:], logf[:], ACT.Ln).then_inc(lnd, 1)

                @block.vector
                def _(dve):
                    step = Steps(dve, steps)
                    TT, TS = nc.vector.tensor_tensor, nc.vector.tensor_scalar
                    dve.wait_ge(wl, 48)
                    step(TT(w3[:, 1, :], w3[:, 1, :], w3[:, 2, :], ALU.add))
                    dve.wait_ge(gates, 1)
                    step(TT(pre[:], k.bank[0][:].rearrange("p (j g) -> p j g", g=16), bc(gbias[:], (P, NT, 16), 1), ALU.add))
                    dve.wait_ge(capped, 2)
                    step(TS(logf[:], logf[:], 1.0, None, ALU.add))
                    dve.wait_ge(lnd, 1)
                    step(TS(logf[:], logf[:], -1.0, None, ALU.mult))
                    dve.wait_ge(cums, 1)
                    step(nc.vector.tensor_copy(flat(lfc[:]), k.bank[1][:, 0:NT * NH]))
                    step(nc.vector.scalar_tensor_tensor(out=a[:], in0=pre[:, :, 0:NH], scalar=CAP, in1=lfc[:],
                                                        op0=ALU.mult, op1=ALU.subtract))
                    dve.wait_ge(aT_done, 1)
                    src = k.bank[2][:, 0:2 * P].rearrange("p (n s) -> p n s", n=4)
                    for c in range(2):
                        step(nc.vector.tensor_copy(aT2[:].rearrange("p h b c s -> p (h b) c s")[:, :, c, :], src))
                    step(TS(gain[:], gain[:], 1.0, None, ALU.add))
                    for half in range(2):
                        for b in range(2):
                            row = aT2[:, half, b, 0, :]
                            step(nc.vector.tensor_tensor_scan(mT[:, half, b, :], row, row, -BIG, ALU.max, ALU.max))
                    dve.wait_ge(aT_back, 1)
                    for h in range(2):
                        for half in range(2):
                            dst = a_b[h * S:(h + 1) * S].rearrange("s (f j b) p -> s f b j p", f=2, b=2)[:, half]
                            frm = k.bank[3][h * S:(h + 1) * S, half * 2 * P:(half + 1) * 2 * P].rearrange(
                                "s (b j p h) -> s b j p h", b=2, j=16, h=2)[:, :, :, :, h]
                            step(nc.vector.tensor_copy(dst, frm))
                    dve.wait_ge(mT_done, 1)
                    step(nc.vector.tensor_copy(flat(m_t[:]), k.bank[4][:, 0:2 * P]))

        km = [sb(f"km{u}", [P, NH, S]) for u in range(2)]
        mb = [sb(f"mb{u}", [P, H2, S]) for u in range(2)]
        e = [sb(f"e{u}", [P, H2, S]) for u in range(2)]
        dm = [sb(f"dm{u}", [P, H2, S]) for u in range(2)]
        pt = [sb(f"pt{u}", [P, H2, P]) for u in range(2)]
        tiny = sb("tiny", [P, 4])
        m_loaded = [sem(f"m_loaded{u}") for u in range(2)]
        km_ready, e_sub, e_ready, d_ready, s_done, p_ready, pv_done, evacuated = [sem(s) for s in (
            "keys_masked", "e_subtracted", "e_ready", "decay_ready", "scores_done", "weights_ready", "pv_done", "evacuated")]
        with nc.Block() as block:
            @block.sync
            def _(sp):
                def body(i):
                    for u in range(2):
                        wait(sp, e_sub, 2 * i + u - 1)
                        for h in range(2):
                            src = d_m.rearrange("b h p t -> (b h) p t")[bass.ds(4 * i + 2 * u + h, 1)]
                            sp.dma_start(mb[u][h * S:(h + 1) * S], src.broadcast_to((S, H2, S))).then_inc(m_loaded[u], 16)
                turns(sp, NT, body)

            @block.gpsimd
            def _(pool):
                def body(i):
                    for u in range(2):
                        b = 2 * i + u
                        wait(pool, s_done, b - 1)
                        nc.gpsimd.tensor_tensor(tiny[:, 2 * u:2 * u + 1], k.ones[:, 0:1], k.ones[:, 0:1], ALU.mult)
                        nc.gpsimd.tensor_tensor(km[u][:], bc(k.ctxT[:, bass.ds(b * S, S)], (P, NH, S), 1),
                                                bc(k.head8[:], (P, NH, S), 2), ALU.mult).then_inc(km_ready, 1)
                turns(pool, NT, body)

            @block.scalar
            def _(act):
                def body(i):
                    for u in range(2):
                        b = 2 * i + u
                        wait(act, p_ready, b - 1)
                        act.wait_ge(e_ready, b + 1)
                        nc.scalar.activation(dm[u][:], e[u][:], ACT.Exp).then_inc(d_ready, 1)
                turns(act, NT, body)

            @block.tensor
            def _(pe):
                def body(i):
                    for u in range(2):
                        b = 2 * i + u
                        pe.wait_ge(km_ready, b + 1)
                        wait(pe, p_ready, b - 1)
                        for q in range(H2):
                            last = nc.tensor.matmul(k.bank[u][:, q * P:(q + 1) * P], km[u][:, 2 * q:2 * q + 2, :].rearrange("p h s -> p (h s)"),
                                                    k.xnT[:, bass.ds(i * P, P)], start=True, stop=True)
                        last.then_inc(s_done, 1)
                    pe.wait_ge(p_ready, 2 * i + 2)
                    wait(pe, evacuated, i)
                    for q in range(H2):
                        for u in range(2):
                            last = nc.tensor.matmul(k.bank[2][:, q * P:(q + 1) * P], pt[u][:, q, :],
                                                    vb[:, bass.ds(((2 * i + u) * H2 + q) * VW, P)],
                                                    start=u == 0, stop=u == 1)
                    last.then_inc(pv_done, 1)
                turns(pe, NT, body)

            @block.vector
            def _(dve):
                def body(i):
                    for u in range(2):
                        b = 2 * i + u
                        dve.wait_ge(m_loaded[u], 32 * (i + 1))
                        wait(dve, d_ready, b - 1)
                        ab = a_b[:].rearrange("p b q -> p (b q)")[:, bass.ds(b * H2, H2)]
                        nc.vector.tensor_tensor(e[u][:], bc(ab, (P, H2, S), 2), mb[u][:], ALU.subtract).then_inc(e_sub, 1)
                        dve.wait_ge(e_sub, b + 1)
                        nc.vector.tensor_tensor(e[u][:], e[u][:], bc(k.causal[:], (P, H2, S), 1), ALU.add).then_inc(e_ready, 1)
                    for u in range(2):
                        b = 2 * i + u
                        dve.wait_ge(s_done, b + 1)
                        wait(dve, pv_done, i)
                        dve.wait_ge(d_ready, b + 1)
                        nc.vector.scalar_tensor_tensor(out=pt[u][:, :, u * S:(u + 1) * S], in0=k.bank[u][:].rearrange("p (q t) -> p q t", q=H2)[:, :, u * S:(u + 1) * S],
                                                       scalar=DH ** -0.5, in1=dm[u][:], op0=ALU.mult, op1=ALU.mult).then_inc(p_ready, 1)
                    dve.wait_ge(pv_done, i + 1)
                    ho = hout[:].rearrange("p j h w -> p (j h w)")
                    nc.vector.tensor_scalar(ho[:, bass.ds(i * H2 * VW, H2 * VW)].rearrange("p (q w) -> p q w", q=H2),
                                            k.bank[2][:].rearrange("p (q w) -> p q w", q=H2)[:, :, 0:VW], 1.0, None,
                                            ALU.mult).then_inc(evacuated, 1)
                for u in range(2):
                    nc.vector.memset(pt[u][:, :, (1 - u) * S:(2 - u) * S], 0.0)
                turns(dve, NT, body)

        with ExitStack() as tmp:
            def tb(name, shape, dt=F32):
                return tmp.enter_context(nc.sbuf_tensor(f"a1_{name}", shape, dt))
            den, em, ss, fac = [tb(n, [P, NT, NH]) for n in ("den", "em", "ss", "fac")]
            sq = tb("sq", [P, NT, NH, DH])
            steps2, expm, squared, rooted = sem("norm_steps"), sem("expm_done"), sem("squared"), sem("rooted")
            num = hout[:, :, :, 0:DH]
            with nc.Block() as block:
                @block.scalar
                def _(act):
                    nc.scalar.activation(sq[:].rearrange("p j h d -> p (j h) d"), hout[:].rearrange("p j h w -> p (j h) w")[:, :, 0:DH],
                                         ACT.Square).then_inc(squared, 1)
                    act.wait_ge(steps2, 1)
                    nc.scalar.activation(em[:], em[:], ACT.Exp, scale=-1.0).then_inc(expm, 1)
                    act.wait_ge(steps2, 9)
                    nc.scalar.activation(fac[:], ss[:], ACT.Sqrt).then_inc(rooted, 1)

                @block.vector
                def _(dve):
                    step = Steps(dve, steps2)
                    TT, TS = nc.vector.tensor_tensor, nc.vector.tensor_scalar
                    step(TT(em[:], lfc[:], m_t[:], ALU.add))
                    step(nc.vector.scalar_tensor_tensor(out=den[:], in0=hout[:, :, :, DH], scalar=-1.0, in1=hout[:, :, :, DH],
                                                        op0=ALU.mult, op1=ALU.max))
                    dve.wait_ge(expm, 1)
                    step(TT(den[:], den[:], em[:], ALU.max))
                    step(TS(den[:], den[:], 5e-5, None, ALU.add))
                    step(nc.vector.reciprocal(den[:], den[:]))
                    dve.wait_ge(squared, 1)
                    step(nc.vector.tensor_reduce(ss[:], sq[:], AX.X, ALU.add))
                    step(TT(ss[:], ss[:], den[:], ALU.mult))
                    step(TT(ss[:], ss[:], den[:], ALU.mult))
                    step(TS(ss[:], ss[:], 1.0 / DH, 1e-6, ALU.mult, ALU.add))
                    dve.wait_ge(rooted, 1)
                    inverse_root(step, nc, fac[:], ss[:], em[:])
                    step(TT(fac[:], fac[:], den[:], ALU.mult))
                    step(TT(sq[:].rearrange("p j h d -> p (j h) d"), hout[:].rearrange("p j h w -> p (j h) w")[:, :, 0:DH],
                            bc(fac[:].rearrange("p j h -> p (j h)"), (P, NT * NH, DH), 2), ALU.mult))
                    hs = sq[:].rearrange("p j h d -> p j (h d)")
                    step(TT(hs, hs, bc(gain[:], (P, NT, D), 1), ALU.mult))
                    step(TT(k.x[:], k.x[:], hs, ALU.add))


def moe_langs(k):
    nc = k.nc
    NL = 4
    with ExitStack() as st:
        def sb(name, shape, dt=F32):
            return st.enter_context(nc.sbuf_tensor(f"f1_{name}", shape, dt))
        w1, w2 = sb("w1", [P, NE * FF]), sb("w2", [P, NE * FF])
        b1, b2 = sb("b1", [P, NE * FF]), sb("b2", [P, NE * D])
        m = Moe(k, "f1", 2, w1, w2, ACT.Gelu, b1, b2)
        wr, br = sb("wr", [P, NE + NL]), sb("br", [P, NE + NL])
        m.lg = sb("lg", [P, NT, NE])
        both = sb("both", [P, NT, NE + NL])
        lp, lmax = sb("lp", [P, NT, NL]), sb("lmax", [P, NT])
        got, steps, expd = k.sem("f1_router_loaded"), k.sem("f1_lang_steps"), k.sem("f1_lang_exp")
        with nc.Block() as block:
            @block.sync
            def _(sp):
                sp.dma_start(wr[:], k.dram["router_lang_wT"]).then_inc(got, 16)
                sp.dma_start(br[:, 0:NE], k.dram["L1_ffn_router_b"].partition_broadcast(P)).then_inc(got, 16)
                sp.dma_start(br[:, NE:], k.dram["L1_ffn_lang_b"].partition_broadcast(P)).then_inc(got, 16)
                sp.wait_ge(got, 48)
        token_logits(k, "f1", both[:], wr[:], NE + NL, br[:])
        with nc.Block() as block:
            @block.scalar
            def _(act):
                act.wait_ge(steps, 2)
                nc.scalar.activation(lp[:], lp[:], ACT.Exp).then_inc(expd, 1)

            @block.vector
            def _(dve):
                step = Steps(dve, steps)
                TT = nc.vector.tensor_tensor
                lang = both[:, :, NE:]
                step(nc.vector.tensor_reduce(lmax[:], lang, AX.X, ALU.max))
                step(TT(lp[:], lang, bc(lmax[:], (P, NT, NL), 2), ALU.subtract))
                dve.wait_ge(expd, 1)
                step(nc.vector.tensor_reduce(lmax[:], lp[:], AX.X, ALU.add))
                step(nc.vector.reciprocal(lmax[:], lmax[:]))
                step(TT(lp[:], lp[:], bc(lmax[:], (P, NT, NL), 2), ALU.mult))
                step(TT(both[:, :, NE:NE + 3], lp[:, :, 0:3], lp[:, :, 1:4], ALU.add))
                step(nc.vector.tensor_copy(both[:, :, NE + 3], lp[:, :, 3]))
                for half in range(2):
                    cols = slice(NL * half, NL * (half + 1))
                    step(nc.vector.scalar_tensor_tensor(out=m.lg[:, :, cols], in0=both[:, :, NE:], scalar=0.1,
                                                        in1=both[:, :, cols], op0=ALU.mult, op1=ALU.add))
        route(k, st, m, expert_weights(k, w1, w2, "L1_ffn_w1", "L1_ffn_w2") + expert_biases(k, b1, b2, "L1_ffn_b1", "L1_ffn_b2"))
        experts(k, m)
        combine(k, m)


def expert_weights(k, w1, w2, n1, n2):
    return [(w1[:].rearrange("d (e f) -> d e f", e=NE), k.dram[n1].rearrange("e d f -> d e f")),
            (w2[:].rearrange("h (e s d) -> h e s d", e=NE, s=HS), k.dram[n2].rearrange("e (s h) d -> h e s d", s=HS))]


def expert_biases(k, b1, b2, n1, n2):
    return [(b1[:], k.dram[n1].rearrange("e f -> (e f)").partition_broadcast(P)),
            (b2[:], k.dram[n2].rearrange("e d -> (e d)").partition_broadcast(P))]


def moe_mlp_router(k):
    nc = k.nc
    with ExitStack() as st:
        def sb(name, shape, dt=F32):
            return st.enter_context(nc.sbuf_tensor(f"f3_{name}", shape, dt))
        w1, w2 = sb("w1", [P, NE * FF]), sb("w2", [P, NE * FF])
        b1, b2 = sb("b1", [P, NE * FF]), sb("b2", [P, NE * D])
        m = Moe(k, "f3", 2, w1, w2, ACT.Relu, b1, b2)
        rw1, rw2 = sb("rw1", [P, FF]), sb("rw2", [P, HS, NE])
        rb1, rb2 = sb("rb1", [P, HS]), sb("rb2", [P, NE])
        m.lg = sb("lg", [P, NT, NE])
        hT = sb("rhT", [P, 2, HS, CH])
        got, up, act_done, lg_done = [k.sem("f3_router_" + s) for s in ("loaded", "up_done", "relu_done", "logits_done")]
        with nc.Block() as block:
            @block.sync
            def _(sp):
                sp.dma_start(rw1[:], k.dram["L3_ffn_rw1"]).then_inc(got, 16)
                sp.dma_start(rw2[:], k.dram["L3_ffn_rw2"].rearrange("(s h) e -> h s e", s=HS)).then_inc(got, 16)
                sp.dma_start(rb1[:], k.dram["rb1T"]).then_inc(got, 16)
                sp.dma_start(rb2[:], k.dram["L3_ffn_rb2"].partition_broadcast(P)).then_inc(got, 16)
                sp.wait_ge(got, 64)

            @block.tensor
            def _(pe):
                pe.wait_ge(got, 64)

                def logits(c):
                    for s in range(HS):
                        pe.wait_ge(act_done, HS * c + s + 1)
                    for t in range(TPC):
                        for s in range(HS):
                            j = c * TPC + t
                            last = nc.tensor.matmul(k.bank[7][:, j * NE:(j + 1) * NE], hT[:, c % 2, s, t * P:(t + 1) * P],
                                                    rw2[:, s, :], start=s == 0, stop=s == HS - 1)
                    last.then_inc(lg_done, 1)
                for c in range(NC):
                    for s in range(HS):
                        if c:
                            pe.wait_ge(act_done, HS * (c - 1) + s + 1)
                        nc.tensor.matmul(k.bank[s][:], rw1[:, s * P:(s + 1) * P], k.xnT[:, c * CH:(c + 1) * CH],
                                         start=True, stop=True).then_inc(up, 1)
                    if c:
                        logits(c - 1)
                logits(NC - 1)

            @block.scalar
            def _(act):
                act.wait_ge(got, 64)
                for c in range(NC):
                    if c >= 2:
                        act.wait_ge(lg_done, c - 1)
                    for s in range(HS):
                        act.wait_ge(up, HS * c + s + 1)
                        nc.scalar.activation(hT[:, c % 2, s, :], k.bank[s][:], ACT.Relu, bias=rb1[:, s:s + 1]).then_inc(act_done, 1)

            @block.vector
            def _(dve):
                dve.wait_ge(lg_done, NC)
                nc.vector.tensor_tensor(m.lg[:], k.bank[7][:, 0:NT * NE].rearrange("p (j e) -> p j e", e=NE),
                                        bc(rb2[:], (P, NT, NE), 1), ALU.add)
        route(k, st, m, expert_weights(k, w1, w2, "L3_ffn_W1", "L3_ffn_W2") + expert_biases(k, b1, b2, "L3_ffn_b1", "L3_ffn_b2"))
        experts(k, m)
        combine(k, m)


def project(k, tag, jobs):
    nc = k.nc
    done, out = k.sem(f"{tag}_projected"), k.sem(f"{tag}_projection_copied")
    with nc.Block() as block:
        @block.tensor
        def _(pe):
            n = 0
            for c in range(NC):
                for _, w, src, _ in jobs:
                    if n >= 4:
                        pe.wait_ge(out, n - 3)
                    nc.tensor.matmul(k.bank[n % 4][:], w, src[:, c * CH:(c + 1) * CH], start=True, stop=True).then_inc(done, 1)
                    n += 1

        @block.scalar
        def _(act):
            n = 0
            for c in range(NC):
                for dst, _, _, bias in jobs:
                    act.wait_ge(done, n + 1)
                    nc.scalar.activation(dst[:, c * CH:(c + 1) * CH], k.bank[n % 4][:], ACT.Identity, bias=bias).then_inc(out, 1)
                    n += 1


def masked_attention(k):
    nc = k.nc
    GP = 8
    G = NT // GP
    SCALE = float(D) ** -0.5
    with ExitStack() as st:
        def sb(name, shape, dt=F32):
            return st.enter_context(nc.sbuf_tensor(f"a2_{name}", shape, dt))

        def sem(name):
            return k.sem(f"a2_{name}")
        w = sb("w", [P, 4, D])
        bcol = sb("bcol", [P, 2])
        brow = sb("brow", [P, 2, D])
        mask_w = sb("mask", [P, NT, S // 4], I32)
        keep, fill = sb("keep", [P, NT, S]), sb("fill", [P, NT, S])
        qT, kT, v = sb("qT", [P, T]), sb("kT", [P, T]), sb("v", [P, NT, D])
        wl, steps = sem("weights_loaded"), sem("mask_steps")
        with nc.Block() as block:
            @block.sync
            def _(sp):
                for i, n in enumerate(("Wq", "Wk", "Wv", "Wo")):
                    sp.dma_start(w[:, i, :], k.dram[f"L2_xattn_{n}"]).then_inc(wl, 16)
                for i, n in enumerate(("bq", "bk")):
                    sp.dma_start(bcol[:, i:i + 1], k.dram[f"L2_xattn_{n}"].rearrange("(d o) -> d o", o=1)).then_inc(wl, 16)
                for i, n in enumerate(("bv", "bo")):
                    sp.dma_start(brow[:, i, :], k.dram[f"L2_xattn_{n}"].partition_broadcast(P)).then_inc(wl, 16)
                for b in range(2):
                    src = k.dram["mask_BxS2_bk0"].rearrange("(j b) w -> b j w", b=2)[b]
                    sp.dma_start(mask_w[b * S:(b + 1) * S], bc(src, (S, NT, S // 4), 0)).then_inc(wl, 16)
                sp.wait_ge(wl, 160)

            @block.vector
            def _(dve):
                step = Steps(dve, steps)
                dve.wait_ge(wl, 160)
                step(nc.vector.tensor_copy(keep[:], mask_w[:].bitcast(U8)))
                step(nc.vector.tensor_scalar(fill[:], keep[:], -1.0, 1e9, ALU.add, ALU.mult))

            @block.gpsimd
            def _(pool):
                pool.wait_ge(wl, 160)
                nc.gpsimd.tensor_tensor(k.x[:], k.x[:], bc(brow[:, 1, :], (P, NT, D), 1), ALU.add)
        project(k, "a2", [(qT, w[:, 0, :], k.xnT, bcol[:, 0:1]), (kT, w[:, 1, :], k.ctxT, bcol[:, 1:2])])
        s = [sb(f"s{u}", [P, GP, S]) for u in range(2)]
        mx, rs = [sb(f"mx{u}", [P, GP]) for u in range(2)], [sb(f"rs{u}", [P, GP]) for u in range(2)]
        pd = sb("pd", [P, GP, P])
        pT = sb("pT", [P, GP, P])
        cT = sb("cT", [P, GP, P])
        v_done, v_out, s_done, s_read, dsteps, expd, pd_ready, turned, pT_ready, pv, cT_ready, o_done, added = [sem(n) for n in (
            "v_done", "v_copied", "scores_done", "scores_read", "dve_steps", "exp_done", "weights_ready", "weights_turned",
            "turned_copied", "pv_done", "pv_copied", "out_done", "x_added")]
        H = GP // TPC
        with nc.Block() as block:
            @block.tensor
            def _(pe):
                for c in range(NC):
                    if c >= 2:
                        pe.wait_ge(v_out, c - 1)
                    for t in range(TPC):
                        j = c * TPC + t
                        last = nc.tensor.matmul(k.bank[c % 2][:, t * P:(t + 1) * P], k.ctxT[:, j * P:(j + 1) * P], w[:, 2, :],
                                                start=True, stop=True)
                    last.then_inc(v_done, 1)
                pe.wait_ge(v_out, NC)

                def scores(g):
                    if g >= 2:
                        pe.wait_ge(s_read, g - 1)
                    for t in range(GP):
                        for b in range(2):
                            at = slice((g * GP + t) * P + b * S, (g * GP + t) * P + (b + 1) * S)
                            last = nc.tensor.matmul(k.bank[g % 2][b * S:(b + 1) * S, t * S:(t + 1) * S], qT[:, at], kT[:, at],
                                                    start=True, stop=True)
                    last.then_inc(s_done, 1)
                scores(0)
                for g in range(G):
                    if g + 1 < G:
                        scores(g + 1)
                    pe.wait_ge(pd_ready, 2 * g + 2)
                    for h in range(H):
                        if g:
                            pe.wait_ge(pT_ready, H * (g - 1) + h + 1)
                        for t in range(TPC):
                            last = nc.tensor.transpose(k.bank[2 + h][:, t * P:(t + 1) * P], pd[:, h * TPC + t, :], k.ident[:])
                        last.then_inc(turned, 1)
                    for h in range(H):
                        pe.wait_ge(pT_ready, H * g + h + 1)
                        if g:
                            pe.wait_ge(cT_ready, H * (g - 1) + h + 1)
                        for t in range(TPC):
                            last = nc.tensor.matmul(k.bank[4 + h][:, t * P:(t + 1) * P], v[:, g * GP + h * TPC + t, :],
                                                    pT[:, h * TPC + t, :], start=True, stop=True)
                        last.then_inc(pv, 1)
                    for h in range(H):
                        pe.wait_ge(cT_ready, H * g + h + 1)
                        if g:
                            pe.wait_ge(added, H * (g - 1) + h + 1)
                        for t in range(TPC):
                            last = nc.tensor.matmul(k.bank[6 + h][:, t * P:(t + 1) * P], cT[:, h * TPC + t, :], w[:, 3, :],
                                                    start=True, stop=True)
                        last.then_inc(o_done, 1)

            @block.scalar
            def _(act):
                for g in range(G):
                    act.wait_ge(dsteps, 5 * g + 3)
                    nc.scalar.activation(s[g % 2][:], s[g % 2][:], ACT.Exp).then_inc(expd, 1)
                    for h in range(H):
                        act.wait_ge(turned, H * g + h + 1)
                        if g:
                            act.wait_ge(pv, H * (g - 1) + h + 1)
                        nc.scalar.copy(flat(pT[:, h * TPC:(h + 1) * TPC, :]), k.bank[2 + h][:]).then_inc(pT_ready, 1)
                    for h in range(H):
                        act.wait_ge(pv, H * g + h + 1)
                        if g:
                            act.wait_ge(o_done, H * (g - 1) + h + 1)
                        nc.scalar.copy(flat(cT[:, h * TPC:(h + 1) * TPC, :]), k.bank[4 + h][:]).then_inc(cT_ready, 1)

            @block.vector
            def _(dve):
                TT = nc.vector.tensor_tensor
                for c in range(NC):
                    dve.wait_ge(v_done, c + 1)
                    TT(v[:, c * TPC:(c + 1) * TPC, :], k.bank[c % 2][:].rearrange("p (t d) -> p t d", t=TPC),
                       bc(brow[:, 0, :], (P, TPC, D), 1), ALU.add).then_inc(v_out, 1)
                step = Steps(dve, dsteps)
                nc.vector.memset(pd[:], 0.0)
                for g in range(G):
                    z, m, r = s[g % 2], mx[g % 2], rs[g % 2]
                    dve.wait_ge(s_done, g + 1)
                    gs = slice(g * GP, (g + 1) * GP)
                    ins = nc.vector.scalar_tensor_tensor(out=z[:], in0=k.bank[g % 2][:].rearrange("p (t s) -> p t s", t=GP),
                                                         scalar=SCALE, in1=keep[:, gs, :], op0=ALU.mult, op1=ALU.mult)
                    ins.then_inc(s_read, 1)
                    dve.wait_ge(s_read, g + 1)
                    step(TT(z[:], z[:], fill[:, gs, :], ALU.add))
                    step(nc.vector.tensor_reduce(m[:], z[:], AX.X, ALU.max))
                    step(TT(z[:], z[:], bc(m[:], (P, GP, S), 2), ALU.subtract))
                    dve.wait_ge(expd, g + 1)
                    step(nc.vector.tensor_reduce(r[:], z[:], AX.X, ALU.add))
                    step(nc.vector.reciprocal(r[:], r[:]))
                    if g:
                        dve.wait_ge(turned, H * g)
                    for b in range(2):
                        h = slice(b * S, (b + 1) * S)
                        TT(pd[h, :, b * S:(b + 1) * S], z[h], bc(r[h], (S, GP, S), 2), ALU.mult).then_inc(pd_ready, 1)
                    for h in range(H):
                        dve.wait_ge(o_done, H * g + h + 1)
                        js = slice(g * GP + h * TPC, g * GP + (h + 1) * TPC)
                        xs = flat(k.x[:, js, :])
                        TT(xs, k.bank[6 + h][:], xs, ALU.add).then_inc(added, 1)


def multi_head_attention(k):
    nc = k.nc
    NH, DH = 16, 8
    NP = NH // 2
    C4 = 4
    VW = 2 * 2 * (DH + 1)
    SCALE = DH ** -0.5
    with ExitStack() as st:
        def sb(name, shape, dt=F32):
            return st.enter_context(nc.sbuf_tensor(f"a3_{name}", shape, dt))

        def sem(name):
            return k.sem(f"a3_{name}")
        qT, kT = sb("qT", [P, T]), k.ctxT
        vb = sb("vb", [P, B * C4 * VW + P])
        vb3 = vb[:, 0:B * C4 * VW].rearrange("s (n w) -> s n w", w=VW)
        drop = sb("drop", [P, B, S])
        wo = sb("wo", [P, 2, 2, D])
        pb = sb("pb", [P, D])
        with ExitStack() as tmp:
            def tb(name, shape, dt=F32):
                return tmp.enter_context(nc.sbuf_tensor(f"a3_{name}", shape, dt))
            wq, wkv = tb("wq", [P, D]), tb("wkv", [P, 2 * D])
            bcol, bv = tb("bcol", [P, 2]), tb("bv", [P, S])
            bvx = tb("bvx", [P, 8, S])
            mask_w = tb("mask", [P, B, S // 4], I32)
            wl, steps, v_done, v_out = sem("weights_loaded"), sem("prep_steps"), sem("v_done"), sem("v_copied")
            with nc.Block() as block:
                @block.sync
                def _(sp):
                    sp.dma_start(wq[:], k.dram["L3_xattn_q_w"]).then_inc(wl, 16)
                    sp.dma_start(wkv[:], k.dram["L3_xattn_kv_w"]).then_inc(wl, 16)
                    sp.dma_start(bcol[:, 0:1], k.dram["L3_xattn_q_b"].rearrange("(d o) -> d o", o=1)).then_inc(wl, 16)
                    sp.dma_start(bcol[:, 1:2], k.dram["L3_xattn_kv_b"][0:D].rearrange("(d o) -> d o", o=1)).then_inc(wl, 16)
                    for p in range(2):
                        src = k.dram["kv_b_byparity"][p]
                        sp.dma_start(bv[p * S:(p + 1) * S], src.partition_broadcast(S)).then_inc(wl, 16)
                    sp.wait_ge(steps, 1)
                    for u in range(2):
                        sp.dma_start(wo[u * S:(u + 1) * S, u], k.dram["proj_w_byparity"].rearrange("h r n -> r h n")).then_inc(wl, 16)
                    sp.dma_start(pb[:], k.dram["L3_xattn_proj_b"].partition_broadcast(P)).then_inc(wl, 16)
                    sp.dma_start(mask_w[:], k.dram["mask_BxS2_bk0"].partition_broadcast(P)).then_inc(wl, 16)
                    sp.wait_ge(wl, 160)

                @block.gpsimd
                def _(pool):
                    nc.gpsimd.memset(wo[:], 0.0)
                    nc.gpsimd.memset(vb[:], 0.0).then_inc(steps, 1)
                    pool.wait_ge(steps, 1)
                    for p in range(2):
                        ones = vb3[p * S:(p + 1) * S, :, p * 18:(p + 1) * 18]
                        ones = ones.rearrange("s n (h w) -> s n h w", h=2)[:, :, :, DH]
                        nc.gpsimd.memset(ones, 1.0).then_inc(steps, 1)
                    pool.wait_ge(wl, 160)
                    pool.wait_ge(steps, 5)
                    nc.gpsimd.tensor_tensor(k.x[:], k.x[:], bc(pb[:], (P, NT, D), 1), ALU.add)

                @block.tensor
                def _(pe):
                    pe.wait_ge(wl, 160)
                    for g in range(B // 8):
                        if g >= 2:
                            pe.wait_ge(v_out, g - 1)
                        for b in range(8):
                            for p in range(2):
                                cols = wkv[:, D:].rearrange("k (c p w) -> k p c w", c=C4, p=2)[:, p]
                                last = nc.tensor.matmul(k.bank[g % 2][p * S:(p + 1) * S, b * S:(b + 1) * S],
                                                        k.ctxT[:, (g * 8 + b) * S:(g * 8 + b + 1) * S], cols, start=True, stop=True)
                        last.then_inc(v_done, 1)

                @block.vector
                def _(dve):
                    dve.wait_ge(wl, 160)
                    TT = nc.vector.tensor_tensor
                    nc.vector.tensor_copy(bvx[:], bc(bv[:], (P, 8, S), 1)).then_inc(steps, 1)
                    nc.vector.tensor_copy(drop[:], mask_w[:].bitcast(U8)).then_inc(steps, 1)
                    dve.wait_ge(steps, 5)
                    nc.vector.tensor_scalar(drop[:], drop[:], -BIG, None, ALU.mult)
                    for g in range(B // 8):
                        dve.wait_ge(v_done, g + 1)
                        for p in range(2):
                            half = slice(p * S, (p + 1) * S)
                            dst = vb3[half, g * 8 * C4:(g + 1) * 8 * C4, p * 18:(p + 1) * 18]
                            last = TT(dst.rearrange("s n (h w) -> s n h w", h=2)[:, :, :, 0:DH],
                                      k.bank[g % 2][half, :].rearrange("s (n h d) -> s n h d", h=2, d=DH),
                                      bvx[half].rearrange("s b (c h d) -> s (b c) h d", h=2, d=DH), ALU.add)
                        last.then_inc(v_out, 1)
            project(k, "a3q", [(qT, wq[:], k.xnT, bcol[:, 0:1])])
            project(k, "a3k", [(kT, wkv[:, 0:D], k.ctxT, bcol[:, 1:2])])

        qm = [sb(f"qm{u}", [P, NH, S]) for u in range(2)]
        z = [sb(f"z{u}", [P, NP, S]) for u in range(2)]
        mx = [sb(f"mx{u}", [P, NP]) for u in range(2)]
        pT = [sb(f"pT{u}", [P, C4, P]) for u in range(2)]
        rs = sb("rs", [P, 2, NP])
        o2 = sb("o2", [P, 2, NP, DH])
        o2T = sb("o2T", [P, P])
        tiny = sb("tiny", [P, 2])
        PB, TB, OTB, OB = k.bank[5], k.bank[4], k.bank[6], k.bank[7]
        qm_ready, s_done, z_read, z_half, z_ready, expd, turned, pT_ready, pv, sums, o2_ready, o2_turned, o2T_ready, o_done, added = [
            sem(s) for s in ("queries_masked", "scores_done", "scores_read", "scores_masked", "shifted", "exp_done", "weights_turned",
                             "turned_copied", "pv_done", "sums_done", "heads_ready", "heads_turned", "heads_copied", "out_done", "x_added")]

        def pairs(eng, body):
            body(0)
            body(1)
            with eng.Fori(2, NT - 1) as m:
                body(m)
            body(NT - 1)

        with nc.Block() as block:
            @block.gpsimd
            def _(pool):
                def body(i):
                    for u in range(2):
                        b = 2 * i + u
                        wait(pool, s_done, b - 1)
                        nc.gpsimd.tensor_tensor(tiny[:, u:u + 1], k.ones[:, 0:1], k.ones[:, 0:1], ALU.mult)
                        nc.gpsimd.tensor_tensor(qm[u][:], bc(qT[:, bass.ds(b * S, S)], (P, NH, S), 1),
                                                bc(k.head16[:], (P, NH, S), 2), ALU.mult).then_inc(qm_ready, 1)
                turns(pool, NT, body)

            @block.tensor
            def _(pe):
                def scores(i, u):
                    b = 2 * i + u
                    pe.wait_ge(qm_ready, b + 1)
                    wait(pe, z_read, b - 1)
                    for p in range(NP):
                        last = nc.tensor.matmul(k.bank[2 * u + p // 4][:, p % 4 * P:(p % 4 + 1) * P],
                                                qm[u][:, 2 * p:2 * p + 2, :].rearrange("d h t -> d (h t)"),
                                                kT[:, bass.ds(i * P, P)], start=True, stop=True)
                    last.then_inc(s_done, 1)

                def turn(i, u):
                    b = 2 * i + u
                    pe.wait_ge(expd, b + 1)
                    wait(pe, pT_ready, b)
                    for c in range(C4):
                        last = nc.tensor.transpose(TB[:, c * P:(c + 1) * P], z[u][:, 2 * c:2 * c + 2, :].rearrange("r p s -> r (p s)"),
                                                   k.ident[:])
                    last.then_inc(turned, 1)

                def weigh(i, u):
                    b = 2 * i + u
                    pe.wait_ge(pT_ready, b + 1)
                    wait(pe, o2_ready, 2 * b)
                    for c in range(C4):
                        last = nc.tensor.matmul(PB[:, c * P:(c + 1) * P], pT[u][:, c, :], vb[:, bass.ds((b * C4 + c) * VW, P)],
                                                start=True, stop=True)
                    last.then_inc(pv, 1)

                def turn_heads(i):
                    pe.wait_ge(o2_ready, 4 * i + 4)
                    wait(pe, o2T_ready, i)
                    nc.tensor.transpose(OTB[:, 0:P], o2[:].rearrange("r u p d -> r (u p d)"), k.ident[:]).then_inc(o2_turned, 1)

                def project_out(i):
                    wait(pe, added, i)
                    pe.wait_ge(o2T_ready, i + 1)
                    for u in range(2):
                        for h in range(2):
                            last = nc.tensor.matmul(OB[u * S:(u + 1) * S, 0:D], o2T[:, h * S:(h + 1) * S], wo[:, u, h, :],
                                                    start=h == 0, stop=h == 1)
                    last.then_inc(o_done, 1)

                def body(m):
                    at = m if isinstance(m, int) else 2
                    scores(m, 1)
                    if at >= 2:
                        project_out(m - 2)
                    if at >= 1:
                        weigh(m - 1, 1)
                    turn(m, 0)
                    if at < NT - 1:
                        scores(m + 1, 0)
                    if at >= 1:
                        turn_heads(m - 1)
                    weigh(m, 0)
                    turn(m, 1)
                scores(0, 0)
                pairs(pe, body)
                weigh(NT - 1, 1)
                project_out(NT - 2)
                turn_heads(NT - 1)
                project_out(NT - 1)

            @block.scalar
            def _(act):
                def exp(i, u):
                    act.wait_ge(z_ready, 2 * i + u + 1)
                    nc.scalar.activation(z[u][:], z[u][:], ACT.Exp).then_inc(expd, 1)

                def copy_turned(i, u):
                    b = 2 * i + u
                    act.wait_ge(turned, b + 1)
                    wait(act, pv, b - 1)
                    nc.scalar.copy(flat(pT[u][:]), TB[:]).then_inc(pT_ready, 1)

                def copy_heads(i):
                    act.wait_ge(o2_turned, i + 1)
                    wait(act, o_done, i)
                    nc.scalar.copy(o2T[:], OTB[:, 0:P]).then_inc(o2T_ready, 1)

                def body(m):
                    at = m if isinstance(m, int) else 2
                    copy_turned(m, 0)
                    exp(m, 1)
                    if at >= 1:
                        copy_heads(m - 1)
                    copy_turned(m, 1)
                    if at < NT - 1:
                        exp(m + 1, 0)
                exp(0, 0)
                pairs(act, body)
                copy_heads(NT - 1)

            @block.vector
            def _(dve):
                TT = nc.vector.tensor_tensor

                def shift(i, u):
                    b = 2 * i + u
                    dve.wait_ge(s_done, b + 1)
                    wait(dve, turned, b - 1)
                    for q in range(2):
                        nc.vector.scalar_tensor_tensor(
                            out=z[u][:, 4 * q:4 * q + 4, :], in0=k.bank[2 * u + q][:].rearrange("r (p s) -> r p s", p=4)[:, :, u * S:(u + 1) * S],
                            scalar=SCALE, in1=bc(flat(drop[:])[:, bass.ds(b * S, S)], (P, 4, S), 1), op0=ALU.mult, op1=ALU.add).then_inc(z_half, 1)
                    dve.wait_ge(z_half, 2 * b + 2)
                    nc.vector.tensor_reduce(mx[u][:], z[u][:], AX.X, ALU.max).then_inc(z_read, 1)
                    dve.wait_ge(z_read, b + 1)
                    TT(z[u][:], z[u][:], bc(mx[u][:], (P, NP, S), 2), ALU.subtract).then_inc(z_ready, 1)

                def divide(i, u):
                    b = 2 * i + u
                    dve.wait_ge(pv, b + 1)
                    wait(dve, o2_turned, i)
                    for h in range(2):
                        half = slice(h * S, (h + 1) * S)
                        own = PB[half, :].rearrange("r (c w) -> r c w", c=C4)[:, :, 0:VW].rearrange("r c (p h w) -> r c p h w", h=2, w=DH + 1)[:, :, :, h, :]
                        sums_of = rs[half, u, :].rearrange("r (c p) -> r c p", c=C4)
                        nc.vector.reciprocal(sums_of, own[:, :, :, DH]).then_inc(sums, 1)
                        dve.wait_ge(sums, 2 * b + h + 1)
                        TT(o2[half, u].rearrange("r (c p) d -> r c p d", c=C4), own[:, :, :, 0:DH],
                           bc(sums_of, (S, C4, 2, DH), 3), ALU.mult).then_inc(o2_ready, 1)

                def add(i):
                    dve.wait_ge(o_done, i + 1)
                    xs = flat(k.x[:])[:, bass.ds(i * D, D)]
                    TT(xs, OB[:, 0:D], xs, ALU.add).then_inc(added, 1)

                def body(m):
                    at = m if isinstance(m, int) else 2
                    shift(m, 1)
                    if at >= 1:
                        divide(m - 1, 1)
                    if at >= 2:
                        add(m - 2)
                    if at < NT - 1:
                        shift(m + 1, 0)
                    divide(m, 0)
                shift(0, 0)
                pairs(dve, body)
                divide(NT - 1, 1)
                add(NT - 2)
                add(NT - 1)


def shared_expert(k):
    nc = k.nc
    SS = 2
    with ExitStack() as st:
        def sb(name, shape, dt=F32):
            return st.enter_context(nc.sbuf_tensor(f"sh_{name}", shape, dt))
        wg, wu, wd = sb("wg", [P, SS * P]), sb("wu", [P, SS * P]), sb("wd", [P, SS, D])
        g, h = sb("g", [P, 2, SS, CH]), sb("h", [P, 2, SS, CH])
        wl, up, gelu, mul, down, added = [k.sem(f"sh_{s}") for s in ("loaded", "up_done", "gelu_done", "multiplied", "down_done", "x_added")]
        with nc.Block() as block:
            @block.sync
            def _(sp):
                sp.dma_start(wg[:], k.dram["SgT"]).then_inc(wl, 16)
                sp.dma_start(wu[:], k.dram["SuT"]).then_inc(wl, 16)
                sp.dma_start(wd[:], k.dram["SdT"].rearrange("(s h) d -> h s d", s=SS)).then_inc(wl, 16)

            @block.tensor
            def _(pe):
                pe.wait_ge(wl, 48)

                def ups(c):
                    for s in range(SS):
                        wait(pe, mul, SS * (c - 1) + s + 1)
                        for w, bank in ((wg, s), (wu, 2 + s)):
                            last = nc.tensor.matmul(k.bank[bank][:], w[:, s * P:(s + 1) * P], k.xnT[:, c * CH:(c + 1) * CH],
                                                    start=True, stop=True)
                        last.then_inc(up, 1)
                ups(0)
                for c in range(NC):
                    if c + 1 < NC:
                        ups(c + 1)
                    pe.wait_ge(mul, SS * (c + 1))
                    wait(pe, added, c - 1)
                    for t in range(TPC):
                        for s in range(SS):
                            last = nc.tensor.matmul(k.bank[4 + c % 2][:, t * P:(t + 1) * P], h[:, c % 2, s, t * P:(t + 1) * P], wd[:, s, :],
                                                    start=s == 0, stop=s == SS - 1)
                    last.then_inc(down, 1)

            @block.scalar
            def _(act):
                for c in range(NC):
                    for s in range(SS):
                        act.wait_ge(up, SS * c + s + 1)
                        wait(act, mul, SS * (c - 2) + s + 1)
                        nc.scalar.activation(g[:, c % 2, s, :], k.bank[s][:], ACT.Gelu).then_inc(gelu, 1)

            @block.vector
            def _(dve):
                def add(c):
                    dve.wait_ge(down, c + 1)
                    xs = flat(k.x[:, c * TPC:(c + 1) * TPC, :])
                    nc.vector.tensor_tensor(xs, k.bank[4 + c % 2][:], xs, ALU.add).then_inc(added, 1)
                for c in range(NC):
                    for s in range(SS):
                        wait(dve, down, c - 1)
                        dve.wait_ge(gelu, SS * c + s + 1)
                        nc.vector.tensor_tensor(h[:, c % 2, s, :], k.bank[2 + s][:], g[:, c % 2, s, :], ALU.mult).then_inc(mul, 1)
                    if c:
                        add(c - 1)
                add(NC - 1)


def expert_choice(k):
    nc = k.nc
    NX, CAP = 16, 2 * T // 16
    CT = CAP // P
    SC = (P, NT, NX)
    SH = (P, NX, NT)
    BITS = 30
    shared_expert(k)
    with ExitStack() as st:
        def sb(name, shape, dt=F32):
            return st.enter_context(nc.sbuf_tensor(f"f2_{name}", shape, dt))

        def sem(name):
            return k.sem(f"f2_{name}")
        token = sb("token", [P, NX, CT], I32)
        with ExitStack() as tmp:
            def tb(name, shape, dt=F32):
                return tmp.enter_context(nc.sbuf_tensor(f"f2_{name}", shape, dt))
            wr, sc, mx = tb("wr", [P, NX]), tb("sc", [P, NT, NX]), tb("mx", [P, NT])
            scT = tb("scT", [P, CH])
            same = tb("same", [P, 8, NX])
            bits_f, bits_i = tb("bits_f", [P, BITS]), tb("bits_i", [P, BITS], I32)
            thr, cand, hit = tb("thr", [P, 1], I32), tb("cand", [P, 1], I32), tb("hit", [P, 1], I32)
            cnt, over = tb("cnt_ge", [P, 1]), tb("over", [P, CH])
            thr_w, thr_bc = tb("thr_w", [P, P]), tb("thr_bc", [P, NX])
            gt, eq, rank, t1 = [tb(n, [P, NT, NX]) for n in ("gt", "eq", "rank", "t1")]
            cs, cum, exc = [tb(n, [P, NX, NT]) for n in ("cs", "cum", "exc")]
            ones_r, left = tb("ones_r", [P, NX * NT]), tb("left", [P, NX])
            ri, qi = tb("ri", [P, NT, NX], I32), tb("qi", [P, NT, NX], I32)
            rf, qf = tb("rf", [P, NT, NX]), tb("qf", [P, NT, NX])
            ohq = tb("ohq", [P, NT * NX, CT])
            val = tb("val", [P, 2, NT * NX * CT], BF16)
            GR = 4
            ohr = tb("ohr", [P, 2, GR, P], BF16)
            tf = tb("tf", [P, NX, CT])
            wl, lg, steps, expd, tables, scT_done, counted, thr_turned, eq_ranked, sel_ranked, oh, used, inv, xst = [sem(s) for s in (
                "router_loaded", "logits_done", "dve_steps", "exp_done", "tables_made", "scores_turned", "counted", "threshold_turned",
                "equal_ranked", "chosen_ranked", "onehots", "onehots_used", "inverted", "rows_stored")]
            search, bsteps = sem("search_steps"), sem("late_steps")
            with nc.Block() as block:
                @block.sync
                def _(sp):
                    sp.dma_start(wr[:], k.dram["gate_wT"]).then_inc(wl, 16)
                    rows = k.d_xs.rearrange("(j p) w -> p j w", p=P)
                    sp.dma_start(rows[:, :, 0:D], k.xn[:]).then_inc(xst, 16)
                    sp.dma_start(k.d_acc.rearrange("(j p) d -> p j d", p=P), bc(k.zeros[:, 0:D], (P, NT, D), 1)).then_inc(xst, 16)
                    sp.wait_ge(steps, 6)
                    sp.dma_start(rows[:, :, D:], sc[:]).then_inc(xst, 16)
                    sp.wait_ge(xst, 48)

                @block.gpsimd
                def _(pool):
                    nc.gpsimd.memset(same[:], 0.0).then_inc(tables, 1)
                    pool.wait_ge(tables, 1)
                    for n in range(8):
                        nc.gpsimd.affine_select(out=same[:], in_=same[:], compare_op=ALU.not_equal, fill=1.0, base=-NX * n,
                                                pattern=[[0, 8], [-1, NX]], channel_multiplier=1).then_inc(tables, 1)
                        pool.wait_ge(tables, n + 2)

                @block.tensor
                def _(pe):
                    pe.wait_ge(wl, 16)
                    for j in range(NT):
                        last = nc.tensor.matmul(k.bank[0][:, j * NX:(j + 1) * NX], k.xnT[:, j * P:(j + 1) * P], wr[:], start=True, stop=True)
                    last.then_inc(lg, 1)
                    pe.wait_ge(steps, 6)
                    for c in range(4):
                        last = nc.tensor.transpose(k.bank[1][:, c * P:(c + 1) * P], flat(sc[:])[:, c * P:(c + 1) * P], k.ident[:])
                    last.then_inc(scT_done, 1)
                    pe.wait_ge(tables, 9)
                    with pe.Fori(0, BITS) as i:
                        pe.wait_ge(search, 4 * i + 2)
                        nc.tensor.matmul(k.bank[2][:, 0:1], same[:].rearrange("p a b -> p (a b)"), cnt[:], start=True, stop=True).then_inc(counted, 1)
                    pe.wait_ge(bsteps, 1)
                    nc.tensor.transpose(k.bank[2][:, 0:P], thr_w[:], k.ident[:]).then_inc(thr_turned, 1)
                    pe.wait_ge(bsteps, 4)
                    for bank, w, src in ((3, k.ones, gt), (4, k.tri, eq), (5, k.ones, eq)):
                        last = nc.tensor.matmul(k.bank[bank][:], w[:], flat(src[:]), start=True, stop=True)
                    last.then_inc(eq_ranked, 1)
                    pe.wait_ge(bsteps, 15)
                    for bank, w in ((6, k.tri), (7, k.ones)):
                        last = nc.tensor.matmul(k.bank[bank][:], w[:], flat(gt[:]), start=True, stop=True)
                    last.then_inc(sel_ranked, 1)

                    def invert(e):
                        for g in range(NT // GR):
                            pe.wait_ge(oh, NT // GR * e + g + 1)
                            for u in range(GR):
                                j = g * GR + u
                                last = nc.tensor.matmul(
                                    k.bank[0][:, bass.ds(e * 2 * CT, 2 * CT)], ohr[:, g % 2, u, :],
                                    val[:, :, bass.ds((j * NX + e) * CT, CT)],
                                    start=j == 0, stop=j == NT - 1)
                            last.then_inc(used, 1)
                    with pe.Fori(0, NX) as e:
                        invert(e)

                @block.scalar
                def _(act):
                    act.wait_ge(steps, 3)
                    nc.scalar.activation(sc[:], sc[:], ACT.Exp).then_inc(expd, 1)

                @block.vector
                def _(dve):
                    step = Steps(dve, steps)
                    TT, TS, RED, CP = nc.vector.tensor_tensor, nc.vector.tensor_scalar, nc.vector.tensor_reduce, nc.vector.tensor_copy
                    dve.wait_ge(lg, 1)
                    step(CP(flat(sc[:]), k.bank[0][:]))
                    step(RED(mx[:], sc[:], AX.X, ALU.max))
                    step(TT(sc[:], sc[:], bc(mx[:], SC, 2), ALU.subtract))
                    dve.wait_ge(expd, 1)
                    step(RED(mx[:], sc[:], AX.X, ALU.add))
                    step(nc.vector.reciprocal(mx[:], mx[:]))
                    step(TT(sc[:], sc[:], bc(mx[:], SC, 2), ALU.mult))
                    for b in range(BITS):
                        nc.vector.memset(bits_f[:, b:b + 1], float(1 << (BITS - 1 - b)))
                    step(nc.vector.memset(thr[:], 0))
                    step(CP(bits_i[:], bits_f[:]))
                    dve.wait_ge(scT_done, 1)
                    step(CP(scT[:], k.bank[1][:]))
                    with dve.Fori(0, BITS) as i:
                        TT(cand[:], thr[:], bits_i[:, bass.ds(i, 1)], ALU.bitwise_or).then_inc(search, 1)
                        dve.wait_ge(search, 4 * i + 1)
                        nc.vector.tensor_scalar(over[:], scT[:], cand[:].bitcast(F32), 0.0, ALU.is_ge, ALU.add,
                                                accum_out=cnt[:]).then_inc(search, 1)
                        dve.wait_ge(counted, i + 1)
                        TS(hit[:], k.bank[2][:, 0:1], CAP - 0.5, bits_f[:, bass.ds(i, 1)], ALU.is_ge, ALU.mult).then_inc(search, 1)
                        dve.wait_ge(search, 4 * i + 3)
                        TT(thr[:], thr[:], hit[:], ALU.bitwise_or).then_inc(search, 1)
                        dve.wait_ge(search, 4 * i + 4)
                    step = Steps(dve, bsteps)
                    step(TS(thr_w[:], k.ones[:], thr[:].bitcast(F32), None, ALU.mult))
                    dve.wait_ge(thr_turned, 1)
                    step(CP(thr_bc[:], k.bank[2][:, 0:NX]))
                    step(TT(gt[:], sc[:], bc(thr_bc[:], SC, 1), ALU.is_gt))
                    step(TT(eq[:], sc[:], bc(thr_bc[:], SC, 1), ALU.is_equal))

                    def rank_of(tri_bank, ones_bank, out):
                        step(CP(cs[:], k.bank[ones_bank][:].rearrange("p (j e) -> p e j", e=NX)))
                        step(nc.vector.tensor_tensor_scan(cum[:].rearrange("p e j -> p (e j)"), ones_r[:],
                                                          cs[:].rearrange("p e j -> p (e j)"), 0.0, ALU.mult, ALU.add))
                        step(TT(exc[:], cum[:], cs[:], ALU.subtract))
                        step(TT(cum[:], exc[:], bc(exc[:, :, 0], SH, 2), ALU.subtract))
                        step(TT(out[:].rearrange("p j e -> p e j"), k.bank[tri_bank][:].rearrange("p (j e) -> p e j", e=NX), cum[:], ALU.add))
                    step(nc.vector.memset(ones_r[:], 1.0))
                    dve.wait_ge(eq_ranked, 1)
                    rank_of(4, 5, rank)
                    step(RED(left[:], k.bank[3][:].rearrange("p (j e) -> p e j", e=NX), AX.X, ALU.add))
                    step(TS(left[:], left[:], -1.0, float(CAP), ALU.mult, ALU.add))
                    step(TT(rank[:], rank[:], bc(left[:], SC, 1), ALU.is_lt))
                    step(TT(eq[:], eq[:], rank[:], ALU.mult))
                    step(TT(gt[:], gt[:], eq[:], ALU.add))
                    dve.wait_ge(sel_ranked, 1)
                    rank_of(6, 7, rank)
                    step(TS(eq[:], gt[:], -1024.0, 1024.0, ALU.mult, ALU.add))
                    step(TT(rank[:], rank[:], gt[:], ALU.mult))
                    step(TT(rank[:], rank[:], eq[:], ALU.add))
                    step(CP(ri[:], rank[:]))
                    step(TS(qi[:], ri[:], 7, None, ALU.arith_shift_right))
                    step(TS(ri[:], ri[:], P - 1, None, ALU.bitwise_and))
                    step(CP(qf[:], qi[:]))
                    step(CP(rf[:], ri[:]))
                    step(TT(ohq[:], bc(k.iota_f[:, 0:CT], (P, NT * NX, CT), 1), bc(qf[:].rearrange("p j e -> p (j e)"), (P, NT * NX, CT), 2), ALU.is_equal))
                    step(TS(val[:, 1, :], flat(ohq[:]), k.pcol[:, 0:1], None, ALU.mult))
                    step(TT(val[:, 0, :].rearrange("p (j w) -> p j w", j=NT), ohq[:].rearrange("p (j e) c -> p j (e c)", e=NX),
                            bc(k.jval[:, 0, :], (P, NT, NX * CT), 2), ALU.mult))
                    frf = rf[:].rearrange("p j e -> p (j e)")

                    def one_hots(e):
                        for g in range(NT // GR):
                            wait(dve, used, NT // GR * e + g - 1)
                            for u in range(GR):
                                last = TS(ohr[:, g % 2, u, :], k.iota[:], frf[:, bass.ds((g * GR + u) * NX + e, 1)], None, ALU.is_equal)
                            last.then_inc(oh, 1)
                    turns(dve, NX, one_hots)
                    dve.wait_ge(used, NT // GR * NX)
                    tok = k.bank[0][:, 0:NX * 2 * CT].rearrange("p (e v c) -> p e v c", v=2, c=CT)
                    step(CP(tf[:], tok[:, :, 0, :]))
                    step(TS(tf[:], tf[:], float(P), -1.0, ALU.mult, ALU.add))
                    step(TT(token[:], tok[:, :, 1, :], tf[:], ALU.add))

        xs = sb("xs", [P, 2, CT, XROW])
        kept = sb("kept", [P, 2, CT])
        xsT = sb("xsT", [P, 2, CAP])
        wg, wu, wd = sb("wg", [P, 2, FF]), sb("wu", [P, 2, FF]), sb("wd", [P, 2, HS, D])
        g, h = sb("g", [P, 2, CAP]), sb("h", [P, HS, CAP])
        y = sb("y", [P, 2, CT, D])
        accb = sb("accb", [P, NT, D])
        gathered = [[sem(f"gathered{u}{t}") for t in range(CT)] for u in range(2)]
        scattered, loaded = sem("scattered"), [sem(f"w_loaded{u}") for u in range(2)]
        turned, xsT_ready, up, gelu, mul, down, y_ready, back, scores_kept = [sem(s) for s in (
            "x_turned", "x_copied", "up_done", "gelu_done", "multiplied", "down_done", "y_ready", "sums_back", "scores_kept")]
        with nc.Block() as block:
            @block.sync
            def _(sp):
                def body(i):
                    for u in range(2):
                        e = 2 * i + u
                        wait(sp, down, e - 1)
                        for dst, name in ((wg[:, u], "WgT"), (wu[:, u], "WuT")):
                            src = k.dram[name].rearrange("e d f -> (e d) f")[bass.ds(e * D, D)]
                            sp.dma_start(dst, src).then_inc(loaded[u], 16)
                        src = k.dram["WdT"].rearrange("e f d -> (e f) d")[bass.ds(e * FF, FF)]
                        sp.dma_start(wd[:, u], src.rearrange("(s h) d -> h s d", s=HS)).then_inc(loaded[u], 16)
                turns(sp, NX // 2, body)
                sp.wait_ge(scattered, 16 * CT * NX)
                sp.dma_start(accb[:], k.d_acc.rearrange("(j p) d -> p j d", p=P)).then_inc(back, 16)

            @block.gpsimd
            def _(pool):
                def gather(e):
                    for t in range(CT):
                        nc.gpsimd.indirect_dma_start(xs[:, e % 2, t, :], None, k.d_xs,
                                                     bass.IndirectOffsetOnAxis(token[:, e, t:t + 1], 0)).then_inc(gathered[e % 2][t], 16)
                gather(0)
                gather(1)
                for e in range(NX):
                    if e + 2 < NX:
                        pool.wait_ge(turned, e + 1)
                        pool.wait_ge(scores_kept, e + 1)
                        gather(e + 2)
                    pool.wait_ge(y_ready, e + 1)
                    wait(pool, scattered, 16 * CT * e)
                    for t in range(CT):
                        nc.gpsimd.indirect_dma_start(k.d_acc, bass.IndirectOffsetOnAxis(token[:, e, t:t + 1], 0), y[:, e % 2, t, :],
                                                     None, compute_op=ALU.add).then_inc(scattered, 16)

            @block.tensor
            def _(pe):
                def turn(i, u):
                    e = 2 * i + u
                    wait(pe, xsT_ready, e)
                    for t in range(CT):
                        pe.wait_ge(gathered[u][t], 16 * (i + 1))
                        last = nc.tensor.transpose(k.bank[0][:, t * P:(t + 1) * P], xs[:, u, t, 0:D], k.ident[:])
                    last.then_inc(turned, 1)

                def up_slice(i, u, s):
                    e = 2 * i + u
                    if s == 0:
                        pe.wait_ge(loaded[u], 48 * (i + 1))
                        pe.wait_ge(xsT_ready, e + 1)
                    wait(pe, mul, HS * e + s - 1)
                    for w, bank in ((wg, 1 + s % 2), (wu, 3 + s % 2)):
                        last = nc.tensor.matmul(k.bank[bank][:], w[:, u, s * P:(s + 1) * P], xsT[:, u, :], start=True, stop=True)
                    last.then_inc(up, 1)

                def body(i, end=False):
                    for u in range(2):
                        e = 2 * i + u
                        ahead = (i + u, 1 - u)
                        more = not (end and u)
                        for s in range(1, HS - 1):
                            up_slice(i, u, s)
                        if more:
                            turn(*ahead)
                        up_slice(i, u, HS - 1)
                        if more:
                            up_slice(*ahead, 0)
                        pe.wait_ge(mul, HS * e + HS)
                        wait(pe, y_ready, e)
                        for t in range(CT):
                            for s in range(HS):
                                last = nc.tensor.matmul(k.bank[5][:, t * P:(t + 1) * P], h[:, s, t * P:(t + 1) * P], wd[:, u, s, :],
                                                        start=s == 0, stop=s == HS - 1)
                        last.then_inc(down, 1)
                turn(0, 0)
                up_slice(0, 0, 0)
                body(0)
                with pe.Fori(1, NX // 2 - 1) as i:
                    body(i)
                body(NX // 2 - 1, end=True)

            @block.scalar
            def _(act):
                def copy(i, u):
                    e = 2 * i + u
                    act.wait_ge(turned, e + 1)
                    wait(act, up, HS * (e - 1))
                    nc.scalar.copy(xsT[:, u, :], k.bank[0][:]).then_inc(xsT_ready, 1)

                def body(i, end=False):
                    for u in range(2):
                        e = 2 * i + u
                        for s in range(HS):
                            if s == HS - 1 and not (end and u):
                                copy(i + u, 1 - u)
                            act.wait_ge(up, HS * e + s + 1)
                            wait(act, mul, HS * e + s - 1)
                            nc.scalar.activation(g[:, s % 2, :], k.bank[1 + s % 2][:], ACT.Gelu).then_inc(gelu, 1)
                copy(0, 0)
                body(0)
                with act.Fori(1, NX // 2 - 1) as i:
                    body(i)
                body(NX // 2 - 1, end=True)

            @block.vector
            def _(dve):
                def body(i):
                    for u in range(2):
                        e = 2 * i + u
                        wait(dve, down, e)
                        for s in range(HS):
                            dve.wait_ge(gelu, HS * e + s + 1)
                            nc.vector.tensor_tensor(h[:, s, :], k.bank[3 + s % 2][:], g[:, s % 2, :], ALU.mult).then_inc(mul, 1)
                            if s == 0:
                                nc.vector.tensor_scalar(kept[:, u, :], xs[:, u, :, bass.ds(e + D, 1)].rearrange("p t o -> p (t o)"),
                                                        1.0, None, ALU.mult).then_inc(scores_kept, 1)
                        dve.wait_ge(down, e + 1)
                        dve.wait_ge(scores_kept, e + 1)
                        wait(dve, scattered, 32 * CT * i + 16 * CT * (u - 1))
                        for t in range(CT):
                            last = nc.vector.tensor_scalar(y[:, u, t, :], k.bank[5][:, t * P:(t + 1) * P],
                                                           kept[:, u, t:t + 1], None, ALU.mult)
                        last.then_inc(y_ready, 1)
                turns(dve, NX // 2, body)
                dve.wait_ge(back, 16)
                nc.vector.tensor_tensor(k.x[:], k.x[:], accb[:], ALU.add)


def store_output(k):
    nc = k.nc
    stored = k.sem("stored")
    with nc.Block() as block:
        @block.sync
        def _(sp):
            sp.dma_start(k.dram["out"].rearrange("b s d -> (b s) d").rearrange("(j p) d -> p j d", p=P), k.x[:]).then_inc(stored, 16)
            sp.wait_ge(stored, 16)


def build(nc, dram):
    with ExitStack() as ctx:
        k = Kernel(nc, ctx, dram)
        load_inputs(k)
        make_tables(k)
        make_attention_tables(k)
        k.d_xn = k.scratch("d_xn", [T + P, D])
        k.d_y = k.scratch("d_y", [YROWS, D])
        k.d_xs = k.scratch("d_xs", [T, XROW])
        k.d_acc = k.scratch("d_acc", [T, D])
        padded = k.sem("pad_rows_zeroed")
        with nc.Block() as block:
            @block.sync
            def _(sp):
                sp.dma_start(k.d_xn[T:T + P, :], k.zeros[:, 0:D]).then_inc(padded, 16)
                sp.wait_ge(padded, 16)
        stages = [autocorrelation_attention, moe_top1, mlstm, moe_langs, masked_attention, expert_choice, multi_head_attention, moe_mlp_router]
        for n, stage in enumerate(stages[:STAGES]):
            layer_norm(k, n)
            stage(k)
            k.end_stage()
        store_output(k)


def lay_out(inputs):
    import numpy as np
    a = {n: np.asarray(v) for n, v in inputs.items()}
    a["ifgate_wT"] = a["L1_xattn_ifgate_w"].T
    a["router_lang_wT"] = np.concatenate([a["L1_ffn_router_w"], a["L1_ffn_lang_w"]]).T
    a["rb1T"] = a["L3_ffn_rb1"].reshape(HS, P).T
    a["kv_b_byparity"] = a["L3_xattn_kv_b"][D:].reshape(4, 2, 16).transpose(1, 0, 2).reshape(2, 64)
    a["proj_w_byparity"] = a["L3_xattn_proj_w"].reshape(8, 2, 8, D).transpose(1, 0, 2, 3).reshape(2, 64, D)
    a["gate_wT"] = a["L2_ffn_gate_w"].T
    for n in ("Sg", "Su", "Sd"):
        a[n + "T"] = a["L2_ffn_" + n].T
    for n in ("Wg", "Wu", "Wd"):
        a[n + "T"] = a["L2_ffn_" + n].transpose(0, 2, 1)
    a["ctxT"] = a["ctx_1024"].reshape(T, D).T
    return a


def kernel(**inputs):
    import numpy as np
    import concourse.bacc as bacc
    from concourse.bass_utils import run_bass_kernel_spmd

    nc = bacc.Bacc("TRN2", target_bir_lowering=False, num_devices=1)
    arrays, dram = {}, {}
    for name, a in lay_out(inputs).items():
        a = np.ascontiguousarray(a)
        if a.dtype == np.bool_:
            a = a.view(np.int32)
        arrays[f"in_{name}"] = a
        dram[name] = nc.dram_tensor(f"in_{name}", a.shape, mybir.dt.from_np(a.dtype), kind="ExternalInput").ap()
    dram["out"] = nc.dram_tensor("out", (B, S, D), F32, kind="ExternalOutput").ap()
    build(nc, dram)
    r = run_bass_kernel_spmd(nc, [arrays], core_ids=[0])
    return r.results[0]["out"]
```
